# Optimizing a Trainium2 kernel written in Bass

```python
import numpy as np
import jax
import jax.numpy as jnp

def _softmax(x, axis=-1):
    return jax.nn.softmax(x, axis=axis)

def _gelu(x):
    return jax.nn.gelu(x, approximate=True)

def _silu(x):
    return jax.nn.silu(x)

def _sigmoid(x):
    return jax.nn.sigmoid(x)

def _layernorm(x, axis=-1, eps=1e-05):
    m = jnp.mean(x, axis=axis, keepdims=True)
    v = jnp.var(x, axis=axis, keepdims=True)
    return (x - m) / jnp.sqrt(v + eps)

def _scatter_add(tgt, idx, src, axis=0):
    return tgt.at[idx].add(src)

def _segment_sum(src, seg, n):
    return jax.ops.segment_sum(src, seg, n)
kernel_name = 'mk_audio_tower_d2_tok_aud1d1024_r4_dcd2c1'

def setup_inputs(seed: int=0):
    np.random.seed(seed)
    _w = jnp.asarray

    def _rec_inputs():
        import jax
        import jax.numpy as jnp
        _rk = jax.random.key(seed)
        x = -9.80646e-05 + 1.00041 * jax.random.normal(jax.random.fold_in(_rk, 1), (16, 4000), jnp.float32)
        return x
    x = _rec_inputs()

    def _L0_tok_setup():
        import jax, jax.numpy as jnp
        import numpy as np
        P = 16
        key = jax.random.key(seed)
        ks = jax.random.split(key, 7)
        B, L = (128, 1024)
        I, H = (512, 256)
        F = 2 * P
        s_in = 1.0 / np.sqrt(F)
        s_mid = 1.0 / np.sqrt(I)
        return {'x': jax.random.normal(ks[0], (B, L), jnp.float32), 'W_h': jax.random.normal(ks[1], (I, F), jnp.float32) * s_in, 'b_h': jax.random.normal(ks[2], (I,), jnp.float32) * s_in, 'W_o': jax.random.normal(ks[3], (H, I), jnp.float32) * s_mid, 'b_o': jax.random.normal(ks[4], (H,), jnp.float32) * s_mid, 'W_r': jax.random.normal(ks[5], (H, F), jnp.float32) * s_in, 'b_r': jax.random.normal(ks[6], (H,), jnp.float32) * s_in}
    _L0_tok_all = _L0_tok_setup()
    _L0_tok_in = {k: v for k, v in _L0_tok_all.items() if k in ('W_h', 'b_h', 'W_o', 'b_o', 'W_r', 'b_r')}
    del _L0_tok_all

    def _L0_attn_setup():
        import jax, jax.numpy as jnp
        import numpy as np
        B, S, E, H, P = (2, 512, 256, 16, 512)
        HD = E // H
        key = jax.random.key(seed)
        ks = jax.random.split(key, 10)
        std = E ** (-0.5)
        x = jax.random.normal(ks[0], (B, S, E), jnp.float32)
        Wq = jax.random.normal(ks[1], (E, E), jnp.float32) * std
        Wk = jax.random.normal(ks[2], (E, E), jnp.float32) * std
        Wv = jax.random.normal(ks[3], (E, E), jnp.float32) * std
        Wo = jax.random.normal(ks[4], (E, E), jnp.float32) * std
        rel_key = jax.random.normal(ks[5], (P, HD), jnp.float32) * 0.02
        z = jnp.zeros((E,), jnp.float32)
        return {'x': x, 'Wq': Wq, 'bq': z, 'Wk': Wk, 'bk': z, 'Wv': Wv, 'bv': z, 'Wo': Wo, 'bo': z, 'rel_key': rel_key}
    _L0_attn_all = _L0_attn_setup()
    _L0_attn_in = {k: v for k, v in _L0_attn_all.items() if k in ('Wq', 'bq', 'Wk', 'bk', 'Wv', 'bv', 'Wo', 'bo', 'rel_key')}
    del _L0_attn_all

    def _L0_ffn_setup():
        import jax, jax.numpy as jnp
        import numpy as np
        B, K, D = (128, 32, 256)
        E = 32
        H = int(D * 0.25)

        def _rsqrt_uniform(key, shape, d):
            bound = d ** (-0.5)
            return jax.random.uniform(key, shape, jnp.float32, -bound, bound)
        key = jax.random.key(seed)
        ks = jax.random.split(key, 7)
        return {'x': jax.random.normal(ks[0], (B, K, D), jnp.float32), 'router_w': _rsqrt_uniform(ks[1], (E, D), D), 'router_b': _rsqrt_uniform(ks[2], (E,), D), 'weights1': _rsqrt_uniform(ks[3], (E, D, H), H), 'bias1': _rsqrt_uniform(ks[4], (E, H), H), 'weights2': _rsqrt_uniform(ks[5], (E, H, D), D), 'bias2': _rsqrt_uniform(ks[6], (E, D), D)}
    _L0_ffn_all = _L0_ffn_setup()
    _L0_ffn_in = {k: v for k, v in _L0_ffn_all.items() if k in ('router_w', 'router_b', 'weights1', 'bias1', 'weights2', 'bias2')}
    del _L0_ffn_all

    def _L1_attn_setup():
        import jax, jax.numpy as jnp
        import numpy as np
        import math
        N_HEAD = 16
        EPS = 1e-06

        def _phi(x, omega):
            m = omega.shape[1]
            proj = jnp.einsum('bhtd,dm->bhtm', x, omega)
            norm_sq_half = 0.5 * jnp.sum(x * x, axis=-1, keepdims=True)
            return jnp.exp(proj - norm_sq_half) / math.sqrt(m)
        key = jax.random.key(seed)
        ks = jax.random.split(key, 4)
        B, T, C = (2, 256, 256)
        d_h, m = (C // N_HEAD, 128)
        x = jax.random.normal(ks[0], (B, T, C), dtype=jnp.float32)
        W_attn = jax.random.normal(ks[1], (C, 3 * C), dtype=jnp.float32) * (1.0 / math.sqrt(C))
        b_attn = jnp.zeros((3 * C,), dtype=jnp.float32)
        W_proj = jax.random.normal(ks[2], (C, C), dtype=jnp.float32) * (1.0 / math.sqrt(C))
        b_proj = jnp.zeros((C,), dtype=jnp.float32)
        omega = jax.random.normal(ks[3], (d_h, m), dtype=jnp.float32)
        return {'x': x, 'W_attn': W_attn, 'b_attn': b_attn, 'W_proj': W_proj, 'b_proj': b_proj, 'omega': omega}
    _L1_attn_all = _L1_attn_setup()
    _L1_attn_in = {k: v for k, v in _L1_attn_all.items() if k in ('W_attn', 'b_attn', 'W_proj', 'b_proj', 'omega')}
    del _L1_attn_all

    def _L1_ffn_setup():
        import jax, jax.numpy as jnp
        import numpy as np
        ALPHA = 1.5
        TEMP = 1.0
        N_ITER = 25
        THRESH = 1e-09

        def entmax_bisect(X, alpha=ALPHA, n_iter=N_ITER):
            d = X.shape[-1]
            inv_am1 = 1.0 / (alpha - 1.0)
            Xs = X * (alpha - 1.0)
            max_val = jnp.max(Xs, axis=-1, keepdims=True)
            tau_lo = max_val - 1.0
            tau_hi = max_val - (1.0 / d) ** (alpha - 1.0)
            f_lo = jnp.sum(jnp.maximum(Xs - tau_lo, 0.0) ** inv_am1, axis=-1, keepdims=True) - 1.0

            def body(i, carry):
                tau_lo, dm, _ = carry
                dm = dm * 0.5
                tau_m = tau_lo + dm
                f_m = jnp.sum(jnp.maximum(Xs - tau_m, 0.0) ** inv_am1, axis=-1, keepdims=True) - 1.0
                tau_lo = jnp.where(f_m * f_lo >= 0.0, tau_m, tau_lo)
                return (tau_lo, dm, tau_m)
            dm0 = tau_hi - tau_lo
            _, _, tau_m = jax.lax.fori_loop(0, n_iter, body, (tau_lo, dm0, tau_lo))
            p = jnp.maximum(Xs - tau_m, 0.0) ** inv_am1
            return p / jnp.sum(p, axis=-1, keepdims=True)
        key = jax.random.key(seed)
        ks = jax.random.split(key, 8)
        B, S, D, E = (2, 256, 256, 8)
        F = 4 * D
        return {'x': jax.random.normal(ks[0], (B, S, D), jnp.float32), 'Wr': jax.random.normal(ks[1], (D, E), jnp.float32) * 0.02, 'br': jnp.zeros((E,), jnp.float32), 'W1': jax.random.normal(ks[2], (E, D, F), jnp.float32) * 0.02, 'b1': jnp.zeros((E, F), jnp.float32), 'W2': jax.random.normal(ks[3], (E, F, D), jnp.float32) * 0.02, 'b2': jnp.zeros((E, D), jnp.float32)}
    _L1_ffn_all = _L1_ffn_setup()
    _L1_ffn_in = {k: v for k, v in _L1_ffn_all.items() if k in ('Wr', 'br', 'W1', 'b1', 'W2', 'b2')}
    del _L1_ffn_all
    return {'x': x, 'L0_tok_W_h': _L0_tok_in['W_h'], 'L0_tok_b_h': _L0_tok_in['b_h'], 'L0_tok_W_o': _L0_tok_in['W_o'], 'L0_tok_b_o': _L0_tok_in['b_o'], 'L0_tok_W_r': _L0_tok_in['W_r'], 'L0_tok_b_r': _L0_tok_in['b_r'], 'L0_attn_Wq': _L0_attn_in['Wq'], 'L0_attn_bq': _L0_attn_in['bq'], 'L0_attn_Wk': _L0_attn_in['Wk'], 'L0_attn_bk': _L0_attn_in['bk'], 'L0_attn_Wv': _L0_attn_in['Wv'], 'L0_attn_bv': _L0_attn_in['bv'], 'L0_attn_Wo': _L0_attn_in['Wo'], 'L0_attn_bo': _L0_attn_in['bo'], 'L0_attn_rel_key': _L0_attn_in['rel_key'], 'L0_ffn_router_w': _L0_ffn_in['router_w'], 'L0_ffn_router_b': _L0_ffn_in['router_b'], 'L0_ffn_weights1': _L0_ffn_in['weights1'], 'L0_ffn_bias1': _L0_ffn_in['bias1'], 'L0_ffn_weights2': _L0_ffn_in['weights2'], 'L0_ffn_bias2': _L0_ffn_in['bias2'], 'L1_attn_W_attn': _L1_attn_in['W_attn'], 'L1_attn_b_attn': _L1_attn_in['b_attn'], 'L1_attn_W_proj': _L1_attn_in['W_proj'], 'L1_attn_b_proj': _L1_attn_in['b_proj'], 'L1_attn_omega': _L1_attn_in['omega'], 'L1_ffn_Wr': _L1_ffn_in['Wr'], 'L1_ffn_br': _L1_ffn_in['br'], 'L1_ffn_W1': _L1_ffn_in['W1'], 'L1_ffn_b1': _L1_ffn_in['b1'], 'L1_ffn_W2': _L1_ffn_in['W2'], 'L1_ffn_b2': _L1_ffn_in['b2']}

def reference(x, L0_tok_W_h, L0_tok_b_h, L0_tok_W_o, L0_tok_b_o, L0_tok_W_r, L0_tok_b_r, L0_attn_Wq, L0_attn_bq, L0_attn_Wk, L0_attn_bk, L0_attn_Wv, L0_attn_bv, L0_attn_Wo, L0_attn_bo, L0_attn_rel_key, L0_ffn_router_w, L0_ffn_router_b, L0_ffn_weights1, L0_ffn_bias1, L0_ffn_weights2, L0_ffn_bias2, L1_attn_W_attn, L1_attn_b_attn, L1_attn_W_proj, L1_attn_b_proj, L1_attn_omega, L1_ffn_Wr, L1_ffn_br, L1_ffn_W1, L1_ffn_b1, L1_ffn_W2, L1_ffn_b2):
    import jax
    import jax.numpy as jnp

    def _L0_tok_ref(x, W_h, b_h, W_o, b_o, W_r, b_r):
        import jax, jax.numpy as jnp
        import numpy as np
        P = 16
        B, L = x.shape
        pad = -L % P
        mask = jnp.ones_like(x)
        if pad > 0:
            x = jnp.pad(x, ((0, 0), (pad, 0)))
            mask = jnp.pad(mask, ((0, 0), (pad, 0)))
        xp = x.reshape(B, -1, P)
        mp = mask.reshape(B, -1, P)
        x_cat = jnp.concatenate([xp, mp], axis=-1)
        hid = jax.nn.silu(jnp.einsum('bnf,if->bni', x_cat, W_h) + b_h)
        out = jnp.einsum('bni,hi->bnh', hid, W_o) + b_o
        res = jnp.einsum('bnf,hf->bnh', x_cat, W_r) + b_r
        return out + res

    def _L0_attn_ref(x, Wq, bq, Wk, bk, Wv, bv, Wo, bo, rel_key):
        import jax, jax.numpy as jnp
        import numpy as np
        B, S, E, H, P = (2, 512, 256, 16, 512)
        HD = E // H
        b, s, e = x.shape
        p, hd = rel_key.shape
        h = e // hd
        scale = hd ** (-0.5)

        def split_heads(t):
            return t.reshape(b, s, h, hd).transpose(0, 2, 1, 3)
        q = split_heads(x @ Wq + bq)
        k = split_heads(x @ Wk + bk)
        v = split_heads(x @ Wv + bv)
        scores = jnp.einsum('bhid,bhjd->bhij', q, k)
        rel = jnp.einsum('bhid,pd->bhip', q, rel_key)
        i = jnp.arange(s)[:, None]
        j = jnp.arange(s)[None, :]
        rel_idx = jnp.clip(j - i + p - 1, 0, p - 1)
        bias = jnp.take_along_axis(rel, jnp.broadcast_to(rel_idx[None, None], (b, h, s, s)), axis=3)
        causal = j <= i
        logits = jnp.where(causal[None, None], (scores + bias) * scale, -jnp.inf)
        attn = jax.nn.softmax(logits, axis=-1)
        out = jnp.einsum('bhij,bhjd->bhid', attn, v)
        out = out.transpose(0, 2, 1, 3).reshape(b, s, e)
        return out @ Wo + bo

    def _L0_ffn_ref(x, router_w, router_b, weights1, bias1, weights2, bias2):
        import jax, jax.numpy as jnp
        import numpy as np
        B, K, D = (128, 32, 256)
        E = 32
        H = int(D * 0.25)

        def _rsqrt_uniform(key, shape, d):
            bound = d ** (-0.5)
            return jax.random.uniform(key, shape, jnp.float32, -bound, bound)
        b, k, d = x.shape
        x_flat = x.reshape(-1, d)
        n = x_flat.shape[0]
        logits = x_flat @ router_w.T + router_b
        routed_idx = jnp.argmax(logits, axis=-1)

        def expert_mlp(w1, b1, w2, b2):
            h = jax.nn.relu(x_flat @ w1 + b1)
            return jax.nn.relu(h @ w2 + b2)
        y_all = jax.vmap(expert_mlp)(weights1, bias1, weights2, bias2)
        out_flat = y_all[routed_idx, jnp.arange(n)]
        return out_flat.reshape(b, k, d)

    def _L1_attn_ref(x, W_attn, b_attn, W_proj, b_proj, omega):
        import jax, jax.numpy as jnp
        import numpy as np
        import math
        N_HEAD = 16
        EPS = 1e-06

        def _phi(x, omega):
            m = omega.shape[1]
            proj = jnp.einsum('bhtd,dm->bhtm', x, omega)
            norm_sq_half = 0.5 * jnp.sum(x * x, axis=-1, keepdims=True)
            return jnp.exp(proj - norm_sq_half) / math.sqrt(m)
        B, T, C = x.shape
        nh = N_HEAD
        d_h = C // nh
        qkv = x @ W_attn + b_attn
        q, k, v = jnp.split(qkv, 3, axis=-1)
        q = q.reshape(B, T, nh, d_h).transpose(0, 2, 1, 3)
        k = k.reshape(B, T, nh, d_h).transpose(0, 2, 1, 3)
        v = v.reshape(B, T, nh, d_h).transpose(0, 2, 1, 3)
        scale = 1.0 / math.sqrt(d_h)
        q = q * scale
        k = k * scale
        phi_q = _phi(q, omega)
        phi_k = _phi(k, omega)
        kv = phi_k[..., :, None] * v[..., None, :]
        S = jnp.cumsum(kv, axis=2)
        Z = jnp.cumsum(phi_k, axis=2)
        num = jnp.einsum('bhtm,bhtmd->bhtd', phi_q, S)
        den = jnp.einsum('bhtm,bhtm->bht', phi_q, Z)[..., None] + EPS
        y = num / den
        y = y.transpose(0, 2, 1, 3).reshape(B, T, C)
        return y @ W_proj + b_proj

    def _L1_ffn_ref(x, Wr, br, W1, b1, W2, b2):
        import jax, jax.numpy as jnp
        import numpy as np
        ALPHA = 1.5
        TEMP = 1.0
        N_ITER = 25
        THRESH = 1e-09

        def entmax_bisect(X, alpha=ALPHA, n_iter=N_ITER):
            d = X.shape[-1]
            inv_am1 = 1.0 / (alpha - 1.0)
            Xs = X * (alpha - 1.0)
            max_val = jnp.max(Xs, axis=-1, keepdims=True)
            tau_lo = max_val - 1.0
            tau_hi = max_val - (1.0 / d) ** (alpha - 1.0)
            f_lo = jnp.sum(jnp.maximum(Xs - tau_lo, 0.0) ** inv_am1, axis=-1, keepdims=True) - 1.0

            def body(i, carry):
                tau_lo, dm, _ = carry
                dm = dm * 0.5
                tau_m = tau_lo + dm
                f_m = jnp.sum(jnp.maximum(Xs - tau_m, 0.0) ** inv_am1, axis=-1, keepdims=True) - 1.0
                tau_lo = jnp.where(f_m * f_lo >= 0.0, tau_m, tau_lo)
                return (tau_lo, dm, tau_m)
            dm0 = tau_hi - tau_lo
            _, _, tau_m = jax.lax.fori_loop(0, n_iter, body, (tau_lo, dm0, tau_lo))
            p = jnp.maximum(Xs - tau_m, 0.0) ** inv_am1
            return p / jnp.sum(p, axis=-1, keepdims=True)
        B, S, D = x.shape
        xt = x.reshape(B * S, D)
        logits = (xt @ Wr + br) / TEMP
        gates = entmax_bisect(logits)
        gates = jnp.where(gates > THRESH, gates, 0.0)
        h = jax.nn.relu(jnp.einsum('td,edf->etf', xt, W1) + b1[:, None, :])
        y = jnp.einsum('etf,efd->etd', h, W2) + b2[:, None, :]
        out = jnp.einsum('etd,te->td', y, gates)
        return out.reshape(B, S, D)
    h = _L0_tok_ref(x, L0_tok_W_h, L0_tok_b_h, L0_tok_W_o, L0_tok_b_o, L0_tok_W_r, L0_tok_b_r)
    h = h + _L0_attn_ref(_layernorm(h, axis=-1), L0_attn_Wq, L0_attn_bq, L0_attn_Wk, L0_attn_bk, L0_attn_Wv, L0_attn_bv, L0_attn_Wo, L0_attn_bo, L0_attn_rel_key)
    h = h + _L0_ffn_ref(_layernorm(h, axis=-1), L0_ffn_router_w, L0_ffn_router_b, L0_ffn_weights1, L0_ffn_bias1, L0_ffn_weights2, L0_ffn_bias2)
    h = h + _L1_attn_ref(_layernorm(h, axis=-1), L1_attn_W_attn, L1_attn_b_attn, L1_attn_W_proj, L1_attn_b_proj, L1_attn_omega)
    h = h + _L1_ffn_ref(_layernorm(h, axis=-1), L1_ffn_Wr, L1_ffn_br, L1_ffn_W1, L1_ffn_b1, L1_ffn_W2, L1_ffn_b2)
    return h

_drawn_inputs = setup_inputs


def setup_inputs(seed=0):
    import zlib

    import numpy as np

    out = dict(_drawn_inputs(seed))
    spreads = {'L0_attn_bq': (0.0, 0.709),
     'L0_attn_bk': (0.0, 0.8),
     'L0_attn_bv': (0.0, 0.1),
     'L0_attn_bo': (0.0, 0.1),
     'L1_attn_b_attn': (0.0, 0.1),
     'L1_attn_b_proj': (0.0, 0.1),
     'L1_ffn_br': (0.0, 0.8),
     'L1_ffn_b1': (0.0, 0.715),
     'L1_ffn_b2': (0.0, 0.334)}
    factors = {'L0_attn_rel_key': 8.0, 'L0_ffn_bias1': 8.0, 'L0_ffn_bias2': 3.366, 'L1_attn_omega': 5.169}
    for name, (base, spread) in spreads.items():
        noise = np.random.default_rng([zlib.crc32(name.encode()), seed]).standard_normal(out[name].shape)
        drawn = base * np.exp(spread * noise) if base else spread * noise
        out[name] = jnp.asarray(drawn.astype(out[name].dtype))
    for name, factor in factors.items():
        out[name] = (out[name] * factor).astype(out[name].dtype)
    return out
```

```python
from contextlib import ExitStack

import numpy as np

import concourse.bass as bass
from concourse import mybir
from concourse.alu_op_type import AluOpType as ALU

F32 = mybir.dt.float32
BF16 = mybir.dt.bfloat16
U32 = mybir.dt.uint32
ACT = mybir.ActivationFunctionType
AX = mybir.AxisListType

B, S, D = 16, 250, 256
PATCH = 16
ROWS = S // 2
TILES = 2 * B
P = 128
DK = D // P
HEADS, HD = 16, 16
GH = P // HD
G = HEADS // GH
HID = 512
NHID = HID // P
XCAT = 2 * PATCH + 2
LN_EPS = 1e-5
MASKED = -1.0e30


def ds(start, size):
    return bass.ds(start, size)


def since(eng, sem, value):
    if not isinstance(value, int) or value > 0:
        eng.wait_ge(sem, value)


def pause(eng, sem, value, paused):
    eng.wait_ge(sem, value)
    eng.sem_inc(paused, 1)


class Stage:

    def __init__(self, nc, name):
        self.nc, self.name, self.ctx = nc, name, ExitStack()

    def __enter__(self):
        return self

    def __exit__(self, *a):
        return self.ctx.__exit__(*a)

    def sb(self, name, shape, dt=F32):
        return self.ctx.enter_context(self.nc.sbuf_tensor(f"{self.name}_{name}", shape, dt))

    def ps(self, name, shape, dt=F32):
        return self.ctx.enter_context(self.nc.psum_tensor(f"{self.name}_{name}", shape, dt))

    def sem(self, name):
        return self.ctx.enter_context(self.nc.semaphore(f"{self.name}_{name}"))


class RowStats:

    def __init__(self, nc, st, H, mv):
        self.nc, self.H, self.mv = nc, H, mv
        self.halves, self.moments = st.sb("halves", [P, 2, 6]), st.sb("moments", [P, 2, 2])
        self.halves_done, self.moments_done = st.sem("halves_done"), st.sem("moments_done")
        self.mv_done, self.paused = st.sem("mv_done"), st.sem("paused")

    def take(self, dve, n, written, count):
        v, rows = self.nc.vector, slice(0, ROWS)
        pause(dve, written, count, self.paused)
        for t in range(2):
            v.bn_stats(self.halves[rows, t, :], self.H[rows, ds(n * 2 + t, 1), :].rearrange("p a d -> p (a d)")).then_inc(self.halves_done, 1)
        pause(dve, self.halves_done, n * 2 + 2, self.paused)
        if not (isinstance(n, int) and n == 0):
            pause(dve, self.mv_done, n, self.paused)
        for t in range(2):
            v.bn_aggr(self.moments[rows, t, :], self.halves[rows, t, :]).then_inc(self.moments_done, 1)
        dve.wait_ge(self.moments_done, n * 2 + 2)
        v.tensor_copy(self.mv[rows, ds(n * 2, 2), :], self.moments[rows, :, :]).then_inc(self.mv_done, 1)


def stage_rstd(nc, name, mv, rstd):
    with Stage(nc, name) as st:
        veps = st.sb("veps", [P, TILES])
        root = st.sb("root", [P, TILES])
        eps_added, rooted, done = st.sem("eps_added"), st.sem("rooted"), st.sem("done")
        with nc.Block() as block:

            @block.vector
            def _(dve):
                nc.vector.tensor_scalar(veps[0:ROWS, :], mv[0:ROWS, :, 1], LN_EPS, None, ALU.add).then_inc(eps_added, 1)
                dve.wait_ge(rooted, 1)
                nc.vector.reciprocal(rstd[0:ROWS, :], root[0:ROWS, :]).then_inc(done, 1)

            @block.scalar
            def _(act):
                act.wait_ge(eps_added, 1)
                nc.scalar.activation(root[0:ROWS, :], veps[0:ROWS, :], ACT.Sqrt).then_inc(rooted, 1)


def sequences(eng, body):
    body(0, 0)
    body(0, 1)
    with eng.Fori(1, B // 2) as it:
        body(it, 0)
        body(it, 1)


def stage_tokens(nc, io, H, mv):
    with Stage(nc, "tok") as st:
        win = st.sb("win", [P, HID + D])
        wout = st.sb("wout", [P, NHID, D])
        xcat = [st.sb(f"xcat{s}", [P, S]) for s in range(2)]
        hid = [st.sb(f"hid{s}", [P, NHID, S]) for s in range(2)]
        stats = RowStats(nc, st, H, mv)
        hid_ps = [st.ps(f"hid_ps{s}", [P, 2, 512]) for s in range(2)]
        out_ps = [st.ps(f"out_ps{s}", [P, 2, D]) for s in range(2)]
        w_loaded, cleared = st.sem("w_loaded"), st.sem("cleared")
        x_loaded = [st.sem(f"x_loaded{s}") for s in range(2)]
        hid_mm, hid_act, out_mm = st.sem("hid_mm"), st.sem("hid_act"), st.sem("out_mm")
        h_done = st.sem("h_done")
        with nc.Block() as block:

            @block.sync
            def _(sp):
                sp.wait_ge(cleared, 1)
                sp.dma_start(win[0:XCAT, :], io["tok_in"][:, :]).then_inc(w_loaded, 16)
                sp.dma_start(wout[:, :, :], io["tok_out"].rearrange("(k p) d -> p k d", p=P)).then_inc(w_loaded, 16)
                sp.wait_ge(cleared, 5)

                def load(it, s):
                    n = it * 2 + s
                    since(sp, out_mm, n - 1)
                    sp.dma_start(xcat[s][0:PATCH, :], io["xt"][:, ds(n * S, S)]).then_inc(x_loaded[s], 16)

                sequences(sp, load)

            @block.vector
            def _(dve):
                nc.vector.memset(win[:, :], 0.0).then_inc(cleared, 1)
                for s in range(2):
                    nc.vector.memset(xcat[s][:, :], 0.0).then_inc(cleared, 1)
                    dve.wait_ge(cleared, 2 * s + 2)
                    nc.vector.memset(xcat[s][0:XCAT, :], 1.0).then_inc(cleared, 1)

                def take(it, s):
                    n = it * 2 + s
                    dve.wait_ge(out_mm, n + 1)
                    nc.vector.tensor_copy(H[0:ROWS, ds(n * 2, 2), :], out_ps[s][0:ROWS, :, :]).then_inc(h_done, 1)
                    stats.take(dve, n, h_done, n + 1)

                sequences(dve, take)

            @block.scalar
            def _(act):
                def silu(it, s):
                    n = it * 2 + s
                    for half in range(2):
                        act.wait_ge(hid_mm, n * 2 + half + 1)
                        since(act, out_mm, n - 1)
                        nc.scalar.activation(hid[s][:, 2 * half:2 * half + 2, :], hid_ps[s][:, half, 0:2 * S].rearrange("p (a t) -> p a t", a=2), ACT.Silu).then_inc(hid_act, 1)

                sequences(act, silu)

            @block.tensor
            def _(pe):
                pe.wait_ge(w_loaded, 32)

                def hidden(it, s):
                    n = it * 2 + s
                    pe.wait_ge(x_loaded[s], it * 16 + 16)
                    for half in range(2):
                        since(pe, hid_act, n * 2 + half - 3)
                        for k in range(2):
                            f = 2 * half + k
                            last = nc.tensor.matmul(hid_ps[s][:, half, k * S:(k + 1) * S], win[:, f * P:(f + 1) * P], xcat[s][:, :], start=True, stop=True)
                        last.then_inc(hid_mm, 1)

                def output(it, s):
                    n = it * 2 + s
                    pe.wait_ge(hid_act, n * 2 + 2)
                    since(pe, h_done, n - 1)
                    for t in range(2):
                        tok = slice(t * ROWS, (t + 1) * ROWS)
                        for f in range(NHID):
                            nc.tensor.matmul(out_ps[s][0:ROWS, t, :], hid[s][:, f, tok], wout[:, f, :], start=(f == 0), stop=False)
                        last = nc.tensor.matmul(out_ps[s][0:ROWS, t, :], xcat[s][:, tok], win[:, HID:HID + D], start=False, stop=True)
                    last.then_inc(out_mm, 1)

                def both(it, s):
                    if s == 0:
                        hidden(it, 0)
                        hidden(it, 1)
                        output(it, 0)
                    else:
                        output(it, 1)

                sequences(pe, both)


QP = 256
BLK = 16
NBLK = QP // BLK
PAIRS = NBLK // 2
XR = P // HD
RELN = S - 2 + 128
RANGE = 512
MINW = P


def pair_width(c):
    return min(max(32 * (c + 1), MINW), S)


def stage_attention(nc, io, H, mv, rstd):
    with Stage(nc, "at") as st:
        sb, ps, sem = st.sb, st.ps, st.sem
        ident = sb("ident", [P, P])
        wq, wk, wv, wo = (sb(n, [P, DK, D]) for n in ("wq", "wk", "wv", "wo"))
        bq, bk = sb("bq", [P, G]), sb("bk", [P, G])
        bv, bo = sb("bv", [P, D]), sb("bo", [P, D])
        relx = sb("relx", [P, RELN])
        cst = sb("cst", [P, GH + BLK + P + 2 * MINW])
        headmask, rowmask = cst[:, 0:GH], cst[:, GH:GH + BLK]
        msel, tri = sb("msel", [P, P], BF16), sb("tri", [P, 2, MINW], BF16)
        xn, xt = sb("xn", [P, 2, D]), sb("xt", [P, DK, S])
        qT = [sb(f"qT{s}", [P, G, QP]) for s in range(2)]
        kT = [sb(f"kT{s}", [P, G, S]) for s in range(2)]
        vpad = [sb(f"vpad{s}", [P, 2, G, GH * (P + HD)]) for s in range(2)]
        qrep = sb("qrep", [P, GH, QP])
        qdiag = [sb(f"qdiag{g}", [P, NBLK, GH, BLK]) for g in range(G)]
        qrow = [sb(f"qrow{g}", [P, NBLK, 2, GH, BLK]) for g in range(G)]
        prob = [sb(f"prob{c}", [P, 2, P if c < PAIRS // 2 else 2 * P]) for c in range(PAIRS)]
        pT = [sb(f"pT{g}", [P, 3, NBLK // 2, P]) for g in range(G)]
        aT = [sb(f"aT{s}", [P, G, QP]) for s in range(2)]
        nmax, total, rtotal = sb("nmax", [P, 4, 2]), sb("total", [P, 4, 2]), sb("rtotal", [P, 4, 2])
        proj, stats = sb("proj", [P, 2, D]), RowStats(nc, st, H, mv)
        score = [ps(f"score{i}", [P, 2, QP]) for i in range(4)]
        turned = [ps(f"turned{i}", [P, 2, 2, P]) for i in range(2)]
        F = [ps(f"front{i}", [P, 512]) for i in range(2)]
        qd = nc.dram_tensor("q_rows", (B, G, P, QP), F32).ap()

        loaded, cleared, consts = sem("loaded"), sem("cleared"), sem("consts")
        xn_done, xt_mm, xt_evac = sem("xn_done"), sem("xt_mm"), sem("xt_evac")
        q_mm, k_mm, v_mm = sem("q_mm"), sem("k_mm"), sem("v_mm")
        q_evac, k_evac, v_evac = sem("q_evac"), sem("k_evac"), sem("v_evac")
        q_stored, qrep_loaded, spread = sem("q_stored"), sem("qrep_loaded"), sem("spread")
        scored, maxed, exped = sem("scored"), sem("maxed"), sem("exped")
        summed, normed = sem("summed"), sem("normed")
        turned_mm, turned_evac = sem("turned_mm"), sem("turned_evac")
        pv_mm, a_evac = sem("pv_mm"), sem("a_evac")
        wo_mm, wo_evac, h_done = sem("wo_mm"), sem("wo_evac"), sem("h_done")

        def side(g, c):
            return {(0, 4): "pv", (0, 6): "wo", (1, 1): "xt", (1, 2): "q", (1, 3): "k", (1, 4): "pv", (1, 6): "v"}.get((g, c))

        def schedule(it, s, first, last):
            n = it * 2 + s
            for g in range(G):
                for c in range(PAIRS):
                    step = side(g, c)
                    if first and g == 0:
                        step = None
                    if last and step in ("xt", "q", "k", "v"):
                        step = None
                    yield g, c, n * 16 + g * PAIRS + c, step

        def run(eng, start, body, finish):
            start()
            body(0, 0, True, False)
            body(0, 1, False, False)
            with eng.Fori(1, B // 2 - 1) as it:
                body(it, 0, False, False)
                body(it, 1, False, False)
            body(B // 2 - 1, 0, False, False)
            body(B // 2 - 1, 1, False, True)
            finish()

        with nc.Block() as block:

            @block.sync
            def _(sp):
                w = lambda k: io[k].rearrange("(k p) d -> p k d", p=P)
                sp.dma_start(ident[:, :], io["ident"]).then_inc(loaded, 16)
                for t, k in ((wq, "at_wq"), (wk, "at_wk"), (wv, "at_wv"), (wo, "at_wo")):
                    sp.dma_start(t[:, :, :], w(k)).then_inc(loaded, 16)
                for t, k in ((bq, "at_bq"), (bk, "at_bk"), (relx, "at_relx"), (cst, "at_cst")):
                    sp.dma_start(t[:, :], io[k]).then_inc(loaded, 16)
                sp.dma_start(bv[:, :], io["at_bv"].broadcast_to([P, D])).then_inc(loaded, 16)
                sp.dma_start(bo[:, :], io["at_bo"].broadcast_to([P, D])).then_inc(loaded, 16)

                def copies(it, s):
                    n = it * 2 + s
                    sp.wait_ge(q_evac, n + 1)
                    sp.dma_start(qd[ds(n, 1), :, :, :].rearrange("o g p i -> p (o g) i"), qT[s][:, :, :]).then_inc(q_stored, 16)
                    sp.wait_ge(q_stored, n * 16 + 16)
                    for g in range(G):
                        since(sp, spread, (n * 2 + g) * 3)
                        for r in range(XR):
                            sp.dma_start(qrep[r * HD:(r + 1) * HD, :, :],
                                         qd[ds(n, 1), g, :, :].rearrange("o (h d) i -> d (o h) i", d=HD)).then_inc(qrep_loaded, 16)

                sequences(sp, copies)

            @block.gpsimd
            def _(pool):
                for v in vpad:
                    nc.gpsimd.memset(v[:, :, :, :], 0.0).then_inc(cleared, 1)
                for t in qrow:
                    nc.gpsimd.memset(t[:, :, :, :, :], 0.0).then_inc(cleared, 1)
                pool.wait_ge(loaded, 16 * 11)

                def spreads(it, s):
                    n = it * 2 + s
                    for g in range(G):
                        u = n * 2 + g
                        pool.wait_ge(q_evac, n + 1)
                        since(pool, scored, (u - 1) * PAIRS)
                        nc.gpsimd.tensor_tensor(
                            qdiag[g][:, :, :, :],
                            qT[s][:, g, :].rearrange("p (a r) -> p a r", r=BLK).unsqueeze(2).broadcast_to([P, NBLK, GH, BLK]),
                            headmask.unsqueeze(1).unsqueeze(3).broadcast_to([P, NBLK, GH, BLK]), ALU.mult).then_inc(spread, 1)
                        pool.wait_ge(qrep_loaded, (n * 2 + g + 1) * 16 * XR)
                        for kt in range(2):
                            nc.gpsimd.tensor_tensor(
                                qrow[g][:, :, kt, :, kt * XR:(kt + 1) * XR],
                                qrep[:, :, :].rearrange("p h (a k r) -> p k a h r", k=2, r=XR)[:, kt, :, :, :],
                                rowmask[:, kt * XR:(kt + 1) * XR].unsqueeze(1).unsqueeze(1).broadcast_to([P, NBLK, GH, XR]), ALU.mult).then_inc(spread, 1)

                pool.wait_ge(cleared, 4)
                sequences(pool, spreads)

            @block.vector
            def _(dve):
                def normalise(m):
                    since(dve, xt_mm, m)
                    for t in range(2):
                        nc.vector.tensor_scalar(xn[0:ROWS, t, :], H[0:ROWS, ds(m * 2 + t, 1), :].rearrange("p a d -> p (a d)"),
                                                mv[0:ROWS, ds(m * 2 + t, 1), 0:1].rearrange("p a o -> p (a o)"), rstd[0:ROWS, ds(m * 2 + t, 1)],
                                                ALU.subtract, ALU.mult).then_inc(xn_done, 1)

                def k_out(s, m):
                    dve.wait_ge(k_mm, m + 1)
                    since(dve, scored, (m - 1) * G * PAIRS)
                    nc.vector.tensor_tensor(kT[s][:, :, :], F[1][:, 0:G * S].rearrange("p (g t) -> p g t", g=G),
                                            bk[:, :].unsqueeze(2).broadcast_to([P, G, S]), ALU.add).then_inc(k_evac, 1)

                def v_out(s, m):
                    dve.wait_ge(v_mm, m + 1)
                    since(dve, pv_mm, m * 2 - 2)
                    for jt, rows in ((0, P), (1, S - P)):
                        for g in range(G):
                            dst = vpad[s][0:rows, jt, g, :].rearrange("p (h c) -> p h c", h=GH)[:, :, 0:HD]
                            nc.vector.tensor_tensor(dst, F[0][0:rows, jt * D + g * P:jt * D + (g + 1) * P].rearrange("p (h c) -> p h c", h=GH),
                                                    bv[0:rows, g * P:(g + 1) * P].rearrange("p (h c) -> p h c", h=GH), ALU.add).then_inc(v_evac, 1)

                def wo_out(m):
                    dve.wait_ge(wo_mm, m + 1)
                    nc.vector.tensor_tensor(proj[0:ROWS, :, :], F[0][0:ROWS, :].rearrange("p (t d) -> p t d", t=2),
                                            bo[0:ROWS, :].unsqueeze(1).broadcast_to([ROWS, 2, D]), ALU.add).then_inc(wo_evac, 1)
                    dve.wait_ge(wo_evac, m + 1)
                    rows = H[0:ROWS, ds(m * 2, 2), :]
                    nc.vector.tensor_tensor(rows, rows, proj[0:ROWS, :, :], ALU.add).then_inc(h_done, 1)
                    stats.take(dve, m, h_done, m + 1)

                def norm(k, g, c):
                    i, w = c % 4, pair_width(c)
                    dve.wait_ge(exped, k * 2 + 2)
                    nc.vector.reciprocal(rtotal[:, i, :], total[:, i, :]).then_inc(summed, 1)
                    dve.wait_ge(summed, k + 1)
                    for a in range(2):
                        nc.vector.tensor_scalar(prob[c][:, a, 0:w], prob[c][:, a, 0:w], rtotal[:, i, a:a + 1], None, ALU.mult).then_inc(normed, 1)

                def start():
                    for c in range(PAIRS):
                        nc.vector.memset(prob[c][:, :, :], 0.0).then_inc(cleared, 1)
                    for s in range(2):
                        nc.vector.memset(qT[s][:, :, :], 0.0).then_inc(cleared, 1)
                    dve.wait_ge(loaded, 16 * 11)
                    nc.vector.tensor_copy(msel[:, :], cst[:, GH + BLK:GH + BLK + P]).then_inc(consts, 1)
                    nc.vector.tensor_copy(tri[:, :, :], cst[:, GH + BLK + P:GH + BLK + P + 2 * MINW].rearrange("p (a j) -> p a j", a=2)).then_inc(consts, 1)
                    nc.vector.tensor_scalar(bq[:, :], bq[:, :], HD ** -0.5, None, ALU.mult).then_inc(consts, 1)
                    dve.wait_ge(cleared, 14)
                    normalise(0)
                    k_out(0, 0)
                    v_out(0, 0)

                def body(it, s, first, last):
                    n = it * 2 + s
                    for g, c, k, step in schedule(it, s, first, last):
                        if g == 0 and c == 0 and not last:
                            normalise(n + 1)
                        dve.wait_ge(scored, k + 1)
                        nc.vector.tensor_reduce(nmax[:, c % 4, :], score[c % 4][:, :, 0:pair_width(c)], AX.X, ALU.max, negate=True).then_inc(maxed, 1)
                        if not (first and g == 0 and c == 0):
                            norm(k - 1, g, (c - 1) % PAIRS)
                        if step == "k":
                            k_out(1 - s, n + 1)
                        if step == "v":
                            v_out(1 - s, n + 1)
                        if step == "wo":
                            wo_out(n - 1)

                def finish():
                    norm(B * 16 - 1, 1, PAIRS - 1)
                    wo_out(B - 1)

                run(dve, start, body, finish)

            @block.scalar
            def _(act):
                def xt_out(m):
                    act.wait_ge(xt_mm, m + 1)
                    since(act, v_mm, m)
                    nc.scalar.activation(xt[:, :, :], F[1][:, 0:DK * S].rearrange("p (k t) -> p k t", k=DK), ACT.Copy).then_inc(xt_evac, 1)

                def q_out(s, m):
                    act.wait_ge(q_mm, m + 1)
                    since(act, spread, (m - 1) * 6)
                    since(act, q_stored, (m - 1) * 16)
                    for g in range(G):
                        last = nc.scalar.activation(qT[s][:, g, 0:S], F[0][:, g * S:(g + 1) * S], ACT.Identity, bias=bq[:, g:g + 1], scale=HD ** -0.5)
                    last.then_inc(q_evac, 1)

                def a_out(s, g, m):
                    act.wait_ge(pv_mm, m * 2 + g + 1)
                    since(act, wo_mm, m - 1)
                    nc.scalar.activation(aT[s][:, g, :], F[g][:, 0:QP], ACT.Copy).then_inc(a_evac, 1)

                def turned_out(k, u, g, c):
                    act.wait_ge(turned_mm, k + 1)
                    if c == 0:
                        since(act, pv_mm, u - 1)
                    if c < PAIRS // 2:
                        nc.scalar.activation(pT[g][:, 0:1, 2 * c:2 * c + 2, :], turned[c % 2][:, 0:1, :, :], ACT.Copy).then_inc(turned_evac, 1)
                    else:
                        a = 2 * c - NBLK // 2
                        nc.scalar.activation(pT[g][:, 1:3, a:a + 2, :], turned[c % 2][:, :, :, :], ACT.Copy).then_inc(turned_evac, 1)

                def start():
                    act.wait_ge(consts, 3)
                    act.wait_ge(cleared, 14)
                    xt_out(0)
                    q_out(0, 0)

                def body(it, s, first, last):
                    n = it * 2 + s
                    for g, c, k, step in schedule(it, s, first, last):
                        i, w = c % 4, pair_width(c)
                        act.wait_ge(maxed, k + 1)
                        since(act, turned_mm, k - PAIRS + 1)
                        for a in range(2):
                            nc.scalar.activation(prob[c][:, a, 0:w], score[i][:, a, 0:w], ACT.Exp, bias=nmax[:, i, a:a + 1],
                                                 accum_out=total[:, i, a:a + 1]).then_inc(exped, 1)
                        if not (first and g == 0 and c < 2):
                            turned_out(k - 2, n * 2 + g - (c < 2), (g if c >= 2 else 1 - g), (c - 2) % PAIRS)
                        if step == "xt":
                            xt_out(n + 1)
                        if step == "q":
                            q_out(1 - s, n + 1)
                        if step == "pv":
                            if g == 0:
                                a_out(1 - s, 1, n - 1)
                            else:
                                a_out(s, 0, n)

                def finish():
                    last = B * 16
                    turned_out(last - 2, 2 * B - 1, 1, PAIRS - 2)
                    turned_out(last - 1, 2 * B - 1, 1, PAIRS - 1)
                    a_out(1, 1, B - 1)

                run(act, start, body, finish)

            @block.tensor
            def _(pe):
                def xt_in(m):
                    pe.wait_ge(xn_done, m * 2 + 2)
                    since(pe, a_evac, m * 2 - 2)
                    for k in range(DK):
                        for t in range(2):
                            last = nc.tensor.transpose(F[1][:, k * S + t * ROWS:k * S + (t + 1) * ROWS], xn[0:ROWS, t, k * P:(k + 1) * P], ident[0:ROWS, 0:ROWS])
                    last.then_inc(xt_mm, 1)

                def q_in(m):
                    pe.wait_ge(xt_evac, m + 1)
                    if isinstance(m, int) and m == 1:
                        pe.wait_ge(v_evac, 4)
                    since(pe, wo_evac, m - 1)
                    for g in range(G):
                        for k in range(DK):
                            last = nc.tensor.matmul(F[0][:, g * S:(g + 1) * S], wq[:, k, g * P:(g + 1) * P], xt[:, k, :], start=(k == 0), stop=(k == DK - 1))
                    last.then_inc(q_mm, 1)

                def k_in(m):
                    pe.wait_ge(xt_evac, m + 1)
                    for g in range(G):
                        for k in range(DK):
                            last = nc.tensor.matmul(F[1][:, g * S:(g + 1) * S], wk[:, k, g * P:(g + 1) * P], xt[:, k, :], start=(k == 0), stop=(k == DK - 1))
                    last.then_inc(k_mm, 1)

                def v_in(m):
                    if isinstance(m, int) and m == 0:
                        pe.wait_ge(q_evac, 1)
                    else:
                        pe.wait_ge(a_evac, m * 2 - 1)
                    for jt, rows in ((0, P), (1, S - P)):
                        for k in range(DK):
                            last = nc.tensor.matmul(F[0][0:rows, jt * D:(jt + 1) * D], xt[:, k, jt * P:jt * P + rows], wv[:, k, :], start=(k == 0), stop=(k == DK - 1))
                    last.then_inc(v_mm, 1)

                def pv_in(s, g, m):
                    bank, u = F[g], m * 2 + g
                    pe.wait_ge(turned_evac, (u + 1) * PAIRS)
                    pe.wait_ge(v_evac, m * 4 + 4)
                    if isinstance(m, int) and m == B - 1:
                        pe.wait_ge(wo_evac, B - 1) if g == 0 else pe.wait_ge(k_evac, B)
                    elif g == 1:
                        pe.wait_ge(k_evac, m + 2)
                    else:
                        pe.wait_ge(q_evac, m + 2)
                    for h in range(GH):
                        for jt in range(2):
                            rhs = pT[g][:, 0:2, :, h * BLK:(h + 1) * BLK].rearrange("p b a r -> p (b a) r") if jt == 0 else pT[g][:, 2, :, h * BLK:(h + 1) * BLK]
                            last = nc.tensor.matmul(bank[:, jt * P:QP], vpad[s][:, jt, g, h * P:(h + 1) * P], rhs, start=(h == 0 and jt == 0), stop=(h == GH - 1 and jt == 1))
                    last.then_inc(pv_mm, 1)

                def wo_in(s, m):
                    pe.wait_ge(a_evac, m * 2 + 2)
                    if not (isinstance(m, int) and m == B - 1):
                        pe.wait_ge(v_evac, m * 4 + 8)
                    for t in range(2):
                        for g in range(G):
                            last = nc.tensor.matmul(F[0][0:ROWS, t * D:(t + 1) * D], aT[s][:, g, t * ROWS:(t + 1) * ROWS], wo[:, g, :], start=(g == 0), stop=(g == G - 1))
                    last.then_inc(wo_mm, 1)

                def scores(s, g, c, k, n):
                    if c == 0:
                        pe.wait_ge(spread, (n * 2 + g + 1) * 3)
                        if g == 0:
                            pe.wait_ge(k_evac, n + 1)
                    since(pe, exped, 2 * k - 6)
                    w = pair_width(c)
                    for a in range(2):
                        blk = 2 * c + a
                        out = score[c % 4][:, a, 0:w]
                        nc.tensor.matmul(out, qdiag[g][:, blk, :, :].rearrange("p h r -> p (h r)"), kT[s][:, g, 0:w], start=True, stop=False)
                        for kt in range(2):
                            off = S - 2 - BLK * blk - XR * kt
                            nc.tensor.matmul(out, qrow[g][:, blk, kt, :, :].rearrange("p h r -> p (h r)"), relx[:, off:off + w], start=False, stop=False)
                        last = nc.tensor.matmul(score[c % 4][:, a, 32 * c:w], msel[:, :], tri[:, a, 0:w - 32 * c], start=False, stop=True)
                    last.then_inc(scored, 1)

                def turn(g, c, k):
                    pe.wait_ge(normed, 2 * k + 2)
                    since(pe, turned_evac, k - 1)
                    for jt in range(1 if c < PAIRS // 2 else 2):
                        for a in range(2):
                            last = nc.tensor.transpose(turned[c % 2][:, jt, a, :], prob[c][:, a, jt * P:(jt + 1) * P], ident[:, :])
                    last.then_inc(turned_mm, 1)

                def start():
                    pe.wait_ge(loaded, 16 * 11)
                    xt_in(0)
                    q_in(0)
                    k_in(0)
                    pe.wait_ge(consts, 3)
                    v_in(0)

                def body(it, s, first, last):
                    n = it * 2 + s
                    for g, c, k, step in schedule(it, s, first, last):
                        scores(s, g, c, k, n)
                        if not (first and g == 0 and c < 2):
                            turn(g if c >= 2 else 1 - g, (c - 2) % PAIRS, k - 2)
                        if step == "xt":
                            xt_in(n + 1)
                        if step == "q":
                            q_in(n + 1)
                        if step == "k":
                            k_in(n + 1)
                        if step == "v":
                            v_in(n + 1)
                        if step == "pv" and g == 0:
                            pv_in(1 - s, 1, n - 1)
                        if step == "pv" and g == 1:
                            pv_in(s, 0, n)
                        if step == "wo":
                            wo_in(1 - s, n - 1)

                def finish():
                    last = B * 16
                    turn(1, PAIRS - 2, last - 2)
                    turn(1, PAIRS - 1, last - 1)
                    pv_in(1, 1, B - 1)
                    wo_in(1, B - 1)

                run(pe, start, body, finish)


CHUNK = 2 * S
CTILES = CHUNK // ROWS
NCHUNK = B * S // CHUNK
E0, H0 = 32, 64
PR = E0 * H0 // P


def normalise_rows(nc, H, mv, rstd, dst, tile):
    return nc.vector.tensor_scalar(dst, H[0:ROWS, ds(tile, 1), :].rearrange("p a d -> p (a d)"),
                                   mv[0:ROWS, ds(tile, 1), 0:1].rearrange("p a o -> p (a o)"), rstd[0:ROWS, ds(tile, 1)],
                                   ALU.subtract, ALU.mult)


def chunk_loop(eng, start, body, finish):
    start()
    body(0, 0, False)
    body(0, 1, False)
    with eng.Fori(1, NCHUNK // 2 - 1) as it:
        body(it, 0, False)
        body(it, 1, False)
    body(NCHUNK // 2 - 1, 0, False)
    body(NCHUNK // 2 - 1, 1, True)
    finish()


def stage_routed(nc, io, H, mv, rstd):
    with Stage(nc, "rt") as st:
        sb, ps, sem = st.sb, st.ps, st.sem
        ident = sb("ident", [P, P])
        w1, w2 = sb("w1", [P, DK, E0 * H0]), sb("w2", [P, PR, D])
        b1, b2 = sb("b1", [P, PR]), sb("b2", [P, D])
        wr, br, ids = sb("wr", [P, DK, E0]), sb("br", [P, E0]), sb("ids", [P, E0])
        own = sb("own", [P, PR, P], BF16)
        xn = sb("xn", [P, CTILES, D])
        xt = [sb(f"xt{s}", [P, DK, CHUNK]) for s in range(2)]
        hid = sb("hid", [P, PR, CHUNK])
        logit, top, topid = sb("logit", [P, CTILES, E0]), sb("top", [P, CTILES, 8]), sb("topid", [P, CTILES, 8], U32)
        topf, onehot = sb("topf", [P, CTILES, 8]), sb("onehot", [P, CTILES, E0])
        onehotT = [sb(f"onehotT{s}", [P, CHUNK]) for s in range(2)]
        push = [sb(f"push{s}", [P, CHUNK], BF16) for s in range(2)]
        stats = RowStats(nc, st, H, mv)
        up = [ps(f"up{i}", [P, 512]) for i in range(2)]
        down = [ps(f"down{i}", [P, 2, D]) for i in range(2)]
        xt_ps, logit_ps, hot_ps = ps("xt_ps", [P, DK, 512]), ps("logit_ps", [P, CTILES, E0 * 4]), ps("hot_ps", [P, 512])
        loaded, cleared, own_made = sem("loaded"), sem("cleared"), sem("own_made")
        w1_loaded, w2_loaded = sem("w1_loaded"), sem("w2_loaded")
        xn_done, xt_mm, xt_evac, logit_mm, route, hot_mm, hot_evac, push_made = (
            sem(n) for n in ("xn_done", "xt_mm", "xt_evac", "logit_mm", "route", "hot_mm", "hot_evac", "push_made"))
        up_mm, relued, down_mm, h_done, paused = (sem(n) for n in ("up_mm", "relued", "down_mm", "h_done", "picked"))
        STEPS = 1 + 2 * CTILES + 2

        with nc.Block() as block:

            @block.sync
            def _(sp):
                for t, k in ((ident, "ident"), (b1, "rt_b1"), (b2, "rt_b2")):
                    sp.dma_start(t[:, :], io[k]).then_inc(loaded, 16)
                for t, k in ((br, "rt_br"), (ids, "rt_ids")):
                    sp.dma_start(t[:, :], io[k].broadcast_to([P, E0])).then_inc(loaded, 16)
                sp.dma_start(wr[:, :, :], io["rt_wr"].rearrange("(k p) e -> p k e", p=P)).then_inc(loaded, 16)
                sp.dma_start(hid[:, 0:4, :].rearrange("p a b -> p (a b)")[:, 0:0 + 4 * CHUNK], io["rt_own"][:, 0:4 * CHUNK]).then_inc(loaded, 16)
                sp.dma_start(hid[:, 4, 0:PR * P - 4 * CHUNK], io["rt_own"][:, 4 * CHUNK:PR * P]).then_inc(loaded, 16)
                sp.dma_start(w1[:, :, :], io["rt_w1"].rearrange("(k p) e -> p k e", p=P)).then_inc(w1_loaded, 16)
                sp.dma_start(w2[:, :, :], io["rt_w2"].rearrange("(k p) e -> p k e", p=P)).then_inc(w2_loaded, 16)

            @block.gpsimd
            def _(pool):
                for s in range(2):
                    nc.gpsimd.memset(onehotT[s][:, :], 0.0).then_inc(cleared, 1)
                    nc.gpsimd.memset(push[s][:, :], 0.0).then_inc(cleared, 1)

            @block.vector
            def _(dve):
                def normalise(j):
                    since(dve, xt_mm, j)
                    for t in range(CTILES):
                        normalise_rows(nc, H, mv, rstd, xn[0:ROWS, t, :], j * CTILES + t).then_inc(xn_done, 1)

                def choose(s, j):
                    dve.wait_ge(logit_mm, j + 1)
                    since(dve, hot_mm, j)
                    nc.vector.tensor_tensor(logit[0:ROWS, :, :], logit_ps[0:ROWS, :, 0:E0], br[0:ROWS, :].unsqueeze(1).broadcast_to([ROWS, CTILES, E0]), ALU.add).then_inc(route, 1)
                    pause(dve, route, j * STEPS + 1, paused)
                    for t in range(CTILES):
                        nc.vector.max(top[0:ROWS, t, :], logit[0:ROWS, t, :]).then_inc(route, 1)
                    pause(dve, route, j * STEPS + 1 + CTILES, paused)
                    for t in range(CTILES):
                        nc.vector.max_index(topid[0:ROWS, t, :], top[0:ROWS, t, :], logit[0:ROWS, t, :]).then_inc(route, 1)
                    dve.wait_ge(route, j * STEPS + 1 + 2 * CTILES)
                    nc.vector.tensor_copy(topf[0:ROWS, :, :], topid[0:ROWS, :, :]).then_inc(route, 1)
                    dve.wait_ge(route, j * STEPS + 2 + 2 * CTILES)
                    nc.vector.tensor_tensor(onehot[0:ROWS, :, :], ids[0:ROWS, :].unsqueeze(1).broadcast_to([ROWS, CTILES, E0]),
                                            topf[0:ROWS, :, 0:1].broadcast_to([ROWS, CTILES, E0]), ALU.is_equal).then_inc(route, 1)

                def pushes(s, j):
                    dve.wait_ge(hot_evac, j + 1)
                    nc.vector.tensor_scalar(push[s][0:E0, :], onehotT[s][0:E0, :], -1.0, -MASKED, ALU.add, ALU.mult).then_inc(push_made, 1)

                def add(j):
                    for half in range(2):
                        dve.wait_ge(down_mm, j * 2 + half + 1)
                        rows = H[0:ROWS, ds(j * CTILES + 2 * half, 2), :]
                        nc.vector.scalar_tensor_tensor(rows, down[half][0:ROWS, :, :], 0.0, rows, ALU.max, ALU.add).then_inc(h_done, 1)
                        stats.take(dve, j * 2 + half, h_done, j * 2 + half + 1)

                def start():
                    dve.wait_ge(loaded, 16 * 8)
                    nc.vector.tensor_copy(own[:, :, :].rearrange("p a b -> p (a b)"), hid[:, 0:5, :].rearrange("p a b -> p (a b)")[:, 0:PR * P]).then_inc(own_made, 1)
                    normalise(0)
                    choose(0, 0)
                    dve.wait_ge(cleared, 4)
                    pushes(0, 0)

                def body(it, s, last):
                    j = it * 2 + s
                    if not last:
                        normalise(j + 1)
                        choose(1 - s, j + 1)
                        pushes(1 - s, j + 1)
                    add(j)

                chunk_loop(dve, start, body, lambda: None)

            @block.scalar
            def _(act):
                def xt_out(s, j):
                    act.wait_ge(xt_mm, j + 1)
                    nc.scalar.activation(xt[s][:, :, :], xt_ps[:, :, 0:CHUNK], ACT.Copy).then_inc(xt_evac, 1)

                def hot_out(s, j):
                    act.wait_ge(hot_mm, j + 1)
                    nc.scalar.activation(onehotT[s][0:E0, :], hot_ps[0:E0, 0:CHUNK], ACT.Copy).then_inc(hot_evac, 1)

                def start():
                    xt_out(0, 0)
                    act.wait_ge(cleared, 4)
                    act.wait_ge(own_made, 1)
                    hot_out(0, 0)

                def body(it, s, last):
                    j = it * 2 + s
                    for pr in range(PR):
                        act.wait_ge(up_mm, j * PR + pr + 1)
                        if pr == 0:
                            since(act, down_mm, j * 2)
                        nc.scalar.activation(hid[:, pr, :], up[pr % 2][:, 0:CHUNK], ACT.Relu, bias=b1[:, pr:pr + 1]).then_inc(relued, 1)
                        if pr == 4 and not last:
                            xt_out(1 - s, j + 1)
                        if pr == 12 and not last:
                            hot_out(1 - s, j + 1)

                chunk_loop(act, start, body, lambda: None)

            @block.tensor
            def _(pe):
                def xt_in(j):
                    pe.wait_ge(xn_done, (j + 1) * CTILES)
                    for k in range(DK):
                        for t in range(CTILES):
                            last = nc.tensor.transpose(xt_ps[:, k, t * ROWS:(t + 1) * ROWS], xn[0:ROWS, t, k * P:(k + 1) * P], ident[0:ROWS, 0:ROWS])
                    last.then_inc(xt_mm, 1)

                def logits_in(s, j):
                    pe.wait_ge(xt_evac, j + 1)
                    since(pe, route, (j - 1) * STEPS + 1)
                    for t in range(CTILES):
                        for k in range(DK):
                            last = nc.tensor.matmul(logit_ps[0:ROWS, t, 0:E0], xt[s][:, k, t * ROWS:(t + 1) * ROWS], wr[:, k, :], start=(k == 0), stop=(k == DK - 1))
                    last.then_inc(logit_mm, 1)

                def hot_in(j):
                    pe.wait_ge(route, (j + 1) * STEPS)
                    since(pe, hot_evac, j)
                    for t in range(CTILES):
                        last = nc.tensor.transpose(hot_ps[0:E0, t * ROWS:(t + 1) * ROWS], onehot[0:ROWS, t, :], ident[0:ROWS, 0:ROWS])
                    last.then_inc(hot_mm, 1)

                def start():
                    pe.wait_ge(loaded, 16 * 8)
                    xt_in(0)
                    logits_in(0, 0)
                    hot_in(0)
                    pe.wait_ge(own_made, 1)
                    pe.wait_ge(w1_loaded, 16)

                def body(it, s, last):
                    j = it * 2 + s
                    pe.wait_ge(push_made, j + 1)
                    for pr in range(PR):
                        since(pe, relued, j * PR + pr - 1)
                        for k in range(DK):
                            nc.tensor.matmul(up[pr % 2][:, 0:CHUNK], w1[:, k, pr * P:(pr + 1) * P], xt[s][:, k, :], start=(k == 0), stop=False)
                        nc.tensor.matmul(up[pr % 2][:, 0:CHUNK], own[:, pr, :], push[s][:, :], start=False, stop=True).then_inc(up_mm, 1)
                        if not last:
                            if pr == 4:
                                xt_in(j + 1)
                            if pr == 7:
                                logits_in(1 - s, j + 1)
                            if pr == 12:
                                hot_in(j + 1)
                    if isinstance(j, int) and j == 0:
                        pe.wait_ge(w2_loaded, 16)
                    pe.wait_ge(hot_evac, j + 1)
                    for t in range(CTILES):
                        tok = slice(t * ROWS, (t + 1) * ROWS)
                        out = down[t // 2][0:ROWS, t % 2, :]
                        if t % 2 == 0:
                            since(pe, h_done, j * 2 - 1 + t // 2)
                        nc.tensor.matmul(out, onehotT[s][:, tok], b2[:, :], start=True, stop=False)
                        for pr in range(PR):
                            if t == 0:
                                pe.wait_ge(relued, j * PR + pr + 1)
                            last = nc.tensor.matmul(out, hid[:, pr, tok], w2[:, pr, :], start=False, stop=(pr == PR - 1))
                        if t % 2 == 1:
                            last.then_inc(down_mm, 1)

                chunk_loop(pe, start, body, lambda: None)


QH = 4
NQ = HEADS // QH
HP = QH * HD
M = P
DEN_EPS = 1e-6


def stage_features(nc, io, H, mv, rstd):
    with Stage(nc, "fe") as st:
        sb, ps, sem = st.sb, st.ps, st.sem
        ident = sb("ident", [P, P])
        wq, wk, wv, wo = (sb(n, [P, DK, D]) for n in ("wq", "wk", "wv", "wo"))
        bias, bias4 = sb("bias", [P, 2, G]), sb("bias4", [P, 2, G])
        bv, bo = sb("bv", [P, D]), sb("bo", [P, D])
        omega, causal = sb("omega", [P, QH, M]), sb("causal", [P, S + ROWS])
        xn, xt = sb("xn", [P, 2, D]), sb("xt", [P, DK, S])
        z = [sb(f"z{s}", [P, 2, NQ, S]) for s in range(2)]
        vone = [sb(f"vone{s}", [P, 2, NQ, QH * (P + HD)]) for s in range(2)]
        phi = [sb(f"phi{i}", [P, 2, S]) for i in range(2)]
        att = [sb(f"att{i}", [P, S + ROWS]) for i in range(2)]
        den, yT = sb("den", [P, S]), [sb(f"yT{s}", [P, G, S]) for s in range(2)]
        proj, stats = sb("proj", [P, 2, D]), RowStats(nc, st, H, mv)
        F = [ps(f"front{i}", [P, 512]) for i in range(2)]
        phi_ps = [ps(f"phi_ps{i}", [P, 512]) for i in range(2)]
        att_ps = [ps(f"att_ps{i}", [P, 512]) for i in range(2)]
        av_ps = [ps(f"av_ps{i}", [P, 512]) for i in range(2)]
        loaded, cleared, consts = sem("loaded"), sem("cleared"), sem("consts")
        xn_done, xt_mm, xt_evac = sem("xn_done"), sem("xt_mm"), sem("xt_evac")
        q_mm, k_mm, v_mm, lin_out, sq_out, v_evac = (sem(n) for n in ("q_mm", "k_mm", "v_mm", "lin_out", "sq_out", "v_evac"))
        phi_mm, exped, att_mm, masked, av_mm = (sem(n) for n in ("phi_mm", "exped", "att_mm", "masked", "av_mm"))
        divided, proj_mm, proj_evac, h_done = (sem(n) for n in ("divided", "proj_mm", "proj_evac", "h_done"))
        LIN = 4

        SIDE = {5: "xt", 7: "q", 9: "k", 11: "v"}

        def run(eng, start, body, finish):
            start()
            body(0, 0, True, False)
            body(0, 1, False, False)
            with eng.Fori(1, B // 2 - 1) as it:
                body(it, 0, False, False)
                body(it, 1, False, False)
            body(B // 2 - 1, 0, False, False)
            body(B // 2 - 1, 1, False, True)
            finish()

        with nc.Block() as block:

            @block.sync
            def _(sp):
                sp.dma_start(ident[:, :], io["ident"]).then_inc(loaded, 16)
                for n, t in enumerate((wq, wk, wv)):
                    sp.dma_start(t[:, :, :], io["fe_w"].rearrange("(k p) d -> p k d", p=P)[:, :, n * D:(n + 1) * D]).then_inc(loaded, 16)
                sp.dma_start(wo[:, :, :], io["fe_wo"].rearrange("(k p) d -> p k d", p=P)).then_inc(loaded, 16)
                sp.dma_start(bias[:, :, :], io["fe_bias"].rearrange("p (c g) -> p c g", c=2)).then_inc(loaded, 16)
                sp.dma_start(omega[:, :, :], io["fe_omega"].rearrange("p (h m) -> p h m", h=QH)).then_inc(loaded, 16)
                sp.dma_start(causal[0:ROWS, :], io["fe_causal"]).then_inc(loaded, 16)
                sp.dma_start(bv[:, :], io["fe_bv"].broadcast_to([P, D])).then_inc(loaded, 16)
                sp.dma_start(bo[:, :], io["fe_bo"].broadcast_to([P, D])).then_inc(loaded, 16)

            @block.gpsimd
            def _(pool):
                for s in range(2):
                    nc.gpsimd.memset(vone[s][:, :, :, :], 0.0).then_inc(cleared, 1)
                pool.wait_ge(cleared, 2)
                for s in range(2):
                    for t in range(2):
                        for qt in range(NQ):
                            ones = vone[s][:, t, qt, :].rearrange("p (h c) -> p h c", h=QH)[:, :, HP:HP + HD]
                            nc.gpsimd.memset(ones, 1.0).then_inc(cleared, 1)

            @block.vector
            def _(dve):
                def normalise(m):
                    since(dve, xt_mm, m)
                    for t in range(2):
                        normalise_rows(nc, H, mv, rstd, xn[0:ROWS, t, :], m * 2 + t).then_inc(xn_done, 1)

                def linear(s, m, which, mm):
                    dve.wait_ge(mm, m + 1)
                    dve.wait_ge(sq_out, m * 2 * LIN + (which + 1) * LIN)
                    for g in range(G):
                        for half in range(2):
                            src = slice(half * HP, (half + 1) * HP)
                            nc.vector.tensor_scalar(z[s][0:HP, which, 2 * g + half, :], F[which][src, g * S:(g + 1) * S],
                                                    bias[src, which, g:g + 1], HD ** -0.5, ALU.add, ALU.mult).then_inc(lin_out, 1)

                def v_out(s, m):
                    dve.wait_ge(v_mm, m + 1)
                    since(dve, av_mm, (m - 1) * HEADS)
                    for qt in range(NQ):
                        nc.vector.tensor_tensor(vone[s][0:ROWS, :, qt, :].rearrange("p t (h c) -> p t h c", h=QH)[:, :, :, 0:HD],
                                                F[0][0:ROWS, :].rearrange("p (t q h d) -> p q t h d", t=2, q=NQ, h=QH)[:, qt, :, :, :],
                                                bv[0:ROWS, qt * HP:(qt + 1) * HP].rearrange("p (h d) -> p h d", h=QH).unsqueeze(1).broadcast_to([ROWS, 2, QH, HD]),
                                                ALU.add).then_inc(v_evac, 1)

                def divide(s, m, qt):
                    q = m * NQ + qt
                    dve.wait_ge(av_mm, (q + 1) * QH)
                    since(dve, proj_mm, m - 1)
                    sums = av_ps[qt % 2]
                    nc.vector.tensor_scalar(den[0:HP, :], sums[HP:P, 0:S], DEN_EPS * M, None, ALU.add).then_inc(divided, 1)
                    dve.wait_ge(divided, q * 3 + 1)
                    nc.vector.reciprocal(den[0:HP, :], den[0:HP, :]).then_inc(divided, 1)
                    dve.wait_ge(divided, q * 3 + 2)
                    half = (qt % 2) * HP
                    nc.vector.tensor_tensor(yT[s][half:half + HP, qt // 2, :], sums[0:HP, 0:S], den[0:HP, :], ALU.mult).then_inc(divided, 1)

                def proj_out(m):
                    dve.wait_ge(proj_mm, m + 1)
                    nc.vector.tensor_tensor(proj[0:ROWS, :, :], F[1][0:ROWS, :].rearrange("p (t d) -> p t d", t=2), bo[0:ROWS, :].unsqueeze(1).broadcast_to([ROWS, 2, D]), ALU.add).then_inc(proj_evac, 1)
                    dve.wait_ge(proj_evac, m + 1)
                    rows = H[0:ROWS, ds(m * 2, 2), :]
                    nc.vector.tensor_tensor(rows, rows, proj[0:ROWS, :, :], ALU.add).then_inc(h_done, 1)
                    stats.take(dve, m, h_done, m + 1)

                def mask(k, h):
                    dve.wait_ge(att_mm, k + 1)
                    since(dve, av_mm, k - 1)
                    nc.vector.tensor_tensor(att[h % 2][0:ROWS, :], att_ps[h % 2][0:ROWS, 0:S + ROWS], causal[0:ROWS, :], ALU.mult).then_inc(masked, 1)

                def start():
                    dve.wait_ge(loaded, 16 * 10)
                    nc.vector.tensor_scalar(bias4[:, :, :], bias[:, :, :], HD ** -0.5, None, ALU.mult).then_inc(consts, 1)
                    normalise(0)
                    linear(0, 0, 0, q_mm)
                    linear(0, 0, 1, k_mm)
                    dve.wait_ge(cleared, 2 + 4 * NQ)
                    v_out(0, 0)

                def body(it, s, first, last):
                    n = it * 2 + s
                    for h in range(HEADS):
                        k = n * HEADS + h
                        if h == 0 and not last:
                            normalise(n + 1)
                        if not (first and h < 1):
                            mask(k - 1, (h - 1) % HEADS)
                        if h == 2 and not first:
                            divide(1 - s, n - 1, NQ - 1)
                        if h in (6, 10, 14):
                            divide(s, n, h // 4 - 1)
                        if h == 4 and not first:
                            proj_out(n - 1)
                        if not last:
                            if h == 7:
                                linear(1 - s, n + 1, 0, q_mm)
                            if h == 9:
                                linear(1 - s, n + 1, 1, k_mm)
                            if h == 11:
                                v_out(1 - s, n + 1)

                def finish():
                    mask(B * HEADS - 1, HEADS - 1)
                    divide(1, B - 1, NQ - 1)
                    proj_out(B - 1)

                run(dve, start, body, finish)

            @block.scalar
            def _(act):
                def xt_out(m):
                    act.wait_ge(xt_mm, m + 1)
                    since(act, v_mm, m)
                    nc.scalar.activation(xt[:, :, :], F[1][:, 0:DK * S].rearrange("p (k t) -> p k t", k=DK), ACT.Copy).then_inc(xt_evac, 1)

                def squares(s, m, which, mm):
                    act.wait_ge(mm, m + 1)
                    since(act, phi_mm, (m - 1) * HEADS)
                    for g in range(G):
                        for half in range(2):
                            src = slice(half * HP, (half + 1) * HP)
                            nc.scalar.activation(z[s][HP:P, which, 2 * g + half, :], F[which][src, g * S:(g + 1) * S], ACT.Square,
                                                 bias=bias4[src, which, g:g + 1], scale=HD ** -0.5).then_inc(sq_out, 1)

                def start():
                    act.wait_ge(consts, 1)
                    xt_out(0)
                    squares(0, 0, 0, q_mm)
                    squares(0, 0, 1, k_mm)

                def body(it, s, first, last):
                    n = it * 2 + s
                    for h in range(HEADS):
                        k = n * HEADS + h
                        act.wait_ge(phi_mm, k + 1)
                        since(act, att_mm, k - 1)
                        nc.scalar.activation(phi[h % 2][:, :, :], phi_ps[h % 2][:, 0:2 * S].rearrange("p (c t) -> p c t", c=2), ACT.Exp).then_inc(exped, 1)
                        if not last:
                            if h == 5:
                                xt_out(n + 1)
                            if h == 7:
                                squares(1 - s, n + 1, 0, q_mm)
                            if h == 9:
                                squares(1 - s, n + 1, 1, k_mm)

                run(act, start, body, lambda: None)

            @block.tensor
            def _(pe):
                def xt_in(m):
                    pe.wait_ge(xn_done, m * 2 + 2)
                    since(pe, lin_out, m * 2 * LIN)
                    since(pe, proj_evac, m - 1)
                    for k in range(DK):
                        for t in range(2):
                            last = nc.tensor.transpose(F[1][:, k * S + t * ROWS:k * S + (t + 1) * ROWS], xn[0:ROWS, t, k * P:(k + 1) * P], ident[0:ROWS, 0:ROWS])
                    last.then_inc(xt_mm, 1)

                def qk_in(w, bank, mm, m):
                    pe.wait_ge(xt_evac, m + 1)
                    if bank == 0:
                        since(pe, v_evac, m * NQ)
                    for g in range(G):
                        for k in range(DK):
                            last = nc.tensor.matmul(F[bank][:, g * S:(g + 1) * S], w[:, k, g * P:(g + 1) * P], xt[:, k, :], start=(k == 0), stop=(k == DK - 1))
                    last.then_inc(mm, 1)

                def v_in(m):
                    pe.wait_ge(lin_out, m * 2 * LIN + LIN)
                    for t in range(2):
                        for k in range(DK):
                            last = nc.tensor.matmul(F[0][0:ROWS, t * D:(t + 1) * D], xt[:, k, t * ROWS:(t + 1) * ROWS], wv[:, k, :], start=(k == 0), stop=(k == DK - 1))
                    last.then_inc(v_mm, 1)

                def features(s, n, k, h):
                    if h == 0:
                        pe.wait_ge(lin_out, (n + 1) * 2 * LIN)
                        pe.wait_ge(sq_out, (n + 1) * 2 * LIN)
                    since(pe, exped, k - 1)
                    for c in range(2):
                        last = nc.tensor.matmul(phi_ps[h % 2][:, c * S:(c + 1) * S], omega[:, h % QH, :], z[s][:, c, h // QH, :], start=True, stop=True)
                    last.then_inc(phi_mm, 1)

                def attend(k, h):
                    pe.wait_ge(exped, k + 1)
                    since(pe, masked, k - 1)
                    q, key = phi[h % 2][:, 0, :], phi[h % 2][:, 1, :]
                    nc.tensor.matmul(att_ps[h % 2][0:ROWS, 0:S], key[:, 0:ROWS], q, start=True, stop=True)
                    nc.tensor.matmul(att_ps[h % 2][0:ROWS, S:S + ROWS], key[:, ROWS:S], q[:, ROWS:S], start=True, stop=True).then_inc(att_mm, 1)

                def values(s, n, k, h):
                    pe.wait_ge(masked, k + 1)
                    qt, hl = h // QH, h % QH
                    if h == 0:
                        pe.wait_ge(v_evac, (n + 1) * NQ)
                    if hl == 0:
                        since(pe, divided, (n * NQ + qt - 1) * 3)
                    head = slice(hl * P, (hl + 1) * P)
                    nc.tensor.matmul(av_ps[qt % 2][:, 0:S], vone[s][0:ROWS, 0, qt, head], att[h % 2][0:ROWS, 0:S], start=(hl == 0), stop=False)
                    nc.tensor.matmul(av_ps[qt % 2][:, ROWS:S], vone[s][0:ROWS, 1, qt, head], att[h % 2][0:ROWS, S:S + ROWS], start=False, stop=(hl == QH - 1)).then_inc(av_mm, 1)

                def proj_in(s, m):
                    pe.wait_ge(divided, (m + 1) * NQ * 3)
                    pe.wait_ge(lin_out, (m + 2) * 2 * LIN if not isinstance(m, int) or m < B - 1 else B * 2 * LIN)
                    for t in range(2):
                        for g in range(G):
                            last = nc.tensor.matmul(F[1][0:ROWS, t * D:(t + 1) * D], yT[s][:, g, t * ROWS:(t + 1) * ROWS], wo[:, g, :], start=(g == 0), stop=(g == G - 1))
                    last.then_inc(proj_mm, 1)

                def start():
                    pe.wait_ge(loaded, 16 * 10)
                    xt_in(0)
                    qk_in(wq, 0, q_mm, 0)
                    qk_in(wk, 1, k_mm, 0)
                    v_in(0)

                def body(it, s, first, last):
                    n = it * 2 + s
                    for h in range(HEADS):
                        k = n * HEADS + h
                        features(s, n, k, h)
                        if not (first and h < 1):
                            attend(k - 1, (h - 1) % HEADS)
                        if not (first and h < 2):
                            values(s if h >= 2 else 1 - s, n if h >= 2 else n - 1, k - 2, (h - 2) % HEADS)
                        if h == 4 and not first:
                            proj_in(1 - s, n - 1)
                        if not last and h in SIDE:
                            step = SIDE[h]
                            if step == "xt":
                                xt_in(n + 1)
                            if step == "q":
                                qk_in(wq, 0, q_mm, n + 1)
                            if step == "k":
                                qk_in(wk, 1, k_mm, n + 1)
                            if step == "v":
                                v_in(n + 1)

                def finish():
                    last = B * HEADS
                    attend(last - 1, HEADS - 1)
                    values(1, B - 1, last - 2, HEADS - 2)
                    values(1, B - 1, last - 1, HEADS - 1)
                    proj_in(1, B - 1)

                run(pe, start, body, finish)


E1, F1 = 8, 1024
FT = F1 // P
THRESH = 1e-9
R32 = mybir.dt.float32r


def split_high(eng, high, x):
    return eng.tensor_copy(high, x)


def split_low(eng, low, x, high):
    return eng.tensor_tensor(low, x, high.bitcast(F32), ALU.subtract)


def three(high_low_a, high_low_b):
    (ah, al), (bh, bl) = high_low_a, high_low_b
    return (ah, bh), (ah, bl), (al, bh)


def stage_gates(nc, io, H, mv, rstd, xh, xl, logit, first_load, first_split):
    with Stage(nc, "ga") as st:
        sb, ps, sem = st.sb, st.ps, st.sem
        ident, wr, br = sb("ident", [P, P]), sb("wr", [P, DK, E1]), sb("br", [P, E1])
        xn = [sb(f"xn{s}", [P, CTILES, D]) for s in range(2)]
        xt = [sb(f"xt{s}", [P, DK, CHUNK]) for s in range(2)]
        xt_ps = [ps(f"xt_ps{s}", [P, DK, 512]) for s in range(2)]
        logit_ps = [ps(f"logit_ps{s}", [P, CTILES, P]) for s in range(2)]
        loaded, xn_done, xt_mm, xt_out, high_out, low_out, logit_mm, logit_evac = (
            sem(n) for n in ("loaded", "xn_done", "xt_mm", "xt_out", "high_out", "low_out", "logit_mm", "logit_evac"))

        def run(eng, body, finish=lambda: None):
            body(0, 0, True)
            body(0, 1, False)
            with eng.Fori(1, NCHUNK // 2) as it:
                body(it, 0, False)
                body(it, 1, False)
            finish()

        with nc.Block() as block:

            @block.sync
            def _(sp):
                sp.dma_start(ident[:, :], io["ident"]).then_inc(loaded, 16)
                sp.dma_start(wr[:, :, :], io["ga_wr"].rearrange("(k p) e -> p k e", p=P)).then_inc(loaded, 16)
                sp.dma_start(br[:, :], io["ga_br"].broadcast_to([P, E1])).then_inc(loaded, 16)
                first_load(sp)

            @block.gpsimd
            def _(pool):
                first_split(pool)

            @block.vector
            def _(dve):
                def low_parts(s, j):
                    dve.wait_ge(xt_out, j + 1)
                    dve.wait_ge(high_out, j + 1)
                    tok = ds(j * CHUNK, CHUNK)
                    split_low(nc.vector, xl[:, :, tok], xt_ps[s][:, :, 0:CHUNK], xh[:, :, tok]).then_inc(low_out, 1)

                def logits_out(s, j):
                    dve.wait_ge(logit_mm, j + 1)
                    nc.vector.tensor_tensor(logit[0:ROWS, ds(j * CTILES, CTILES), :], logit_ps[s][0:ROWS, :, 0:E1],
                                            br[0:ROWS, :].unsqueeze(1).broadcast_to([ROWS, CTILES, E1]), ALU.add).then_inc(logit_evac, 1)

                def normalise(s, j):
                    since(dve, xt_mm, j - 1)
                    for t in range(CTILES):
                        normalise_rows(nc, H, mv, rstd, xn[s][0:ROWS, t, :], j * CTILES + t).then_inc(xn_done, 1)

                def body(it, s, first):
                    j = it * 2 + s
                    normalise(s, j)
                    if not first:
                        low_parts(1 - s, j - 1)
                        if not (isinstance(it, int) and it == 0):
                            logits_out(s, j - 2)

                def finish():
                    low_parts(1, NCHUNK - 1)
                    logits_out(0, NCHUNK - 2)
                    logits_out(1, NCHUNK - 1)

                dve.wait_ge(loaded, 48)
                run(dve, body, finish)

            @block.scalar
            def _(act):
                def body(it, s, first):
                    j = it * 2 + s
                    act.wait_ge(xt_mm, j + 1)
                    nc.scalar.activation(xh[:, :, ds(j * CHUNK, CHUNK)], xt_ps[s][:, :, 0:CHUNK], ACT.Copy).then_inc(high_out, 1)
                    since(act, logit_mm, j - 1)
                    nc.scalar.activation(xt[s][:, :, :], xt_ps[s][:, :, 0:CHUNK], ACT.Copy).then_inc(xt_out, 1)

                run(act, body)

            @block.tensor
            def _(pe):
                def logits_in(s, j):
                    pe.wait_ge(xt_out, j + 1)
                    since(pe, logit_evac, j - 1)
                    for t in range(CTILES):
                        for k in range(DK):
                            last = nc.tensor.matmul(logit_ps[s][0:ROWS, t, 0:E1], xt[s][:, k, t * ROWS:(t + 1) * ROWS], wr[:, k, :], start=(k == 0), stop=(k == DK - 1))
                    last.then_inc(logit_mm, 1)

                def body(it, s, first):
                    j = it * 2 + s
                    pe.wait_ge(xn_done, (j + 1) * CTILES)
                    since(pe, low_out, j - 1)
                    for k in range(DK):
                        for t in range(CTILES):
                            last = nc.tensor.transpose(xt_ps[s][:, k, t * ROWS:(t + 1) * ROWS], xn[s][0:ROWS, t, k * P:(k + 1) * P], ident[0:ROWS, 0:ROWS])
                    last.then_inc(xt_mm, 1)
                    if not first:
                        logits_in(1 - s, j - 1)

                pe.wait_ge(loaded, 48)
                run(pe, body, lambda: logits_in(1, NCHUNK - 1))


def entmax(nc, dve, st, chain, root, take_root, logit, gate):
    r, v = slice(0, ROWS), nc.vector
    ranked, cut = st.sb("ranked", [P, TILES, E1]), st.sb("cut", [P, TILES, E1])
    total = st.sb("total", [P, 2, TILES, E1])
    inverse = st.sb("inverse", [P, E1])
    tau, mass, slope = (st.sb(n, [P, TILES]) for n in ("tau", "mass", "slope"))
    wide = lambda t: t[r, :].unsqueeze(2).broadcast_to([ROWS, TILES, E1])
    per_k = inverse[r, :].unsqueeze(1).broadcast_to([ROWS, TILES, E1])
    count = 0

    def step(ins):
        nonlocal count
        count += 1
        ins.then_inc(chain, 1)
        dve.wait_ge(chain, count)

    def over(x):
        step(v.tensor_tensor(cut[r, :, :], x, wide(tau), ALU.subtract))
        step(v.tensor_scalar(cut[r, :, :], cut[r, :, :], 0.0, None, ALU.max))

    for k in range(E1):
        step(v.memset(inverse[:, k:k + 1], 1.0 / (k + 1)))
    for t in range(TILES):
        ins = v.max(ranked[r, t, :], logit[r, t, :])
        count += 1
        ins.then_inc(chain, 1)
    dve.wait_ge(chain, count)
    top = ranked[r, :, 0:1].broadcast_to([ROWS, TILES, E1])
    step(v.tensor_tensor(logit[r, :, :], logit[r, :, :], top, ALU.subtract))
    step(v.tensor_tensor(total[r, 0, :, :], ranked[r, :, :], top, ALU.subtract))
    step(v.tensor_scalar(logit[r, :, :], logit[r, :, :], 0.5, None, ALU.mult))
    step(v.tensor_scalar(ranked[r, :, :], total[r, 0, :, :], 0.5, -1.0, ALU.mult, ALU.max))
    step(v.tensor_copy(total[r, 0, :, :], ranked[r, :, :]))
    step(v.tensor_tensor(total[r, 1, :, :], ranked[r, :, :], ranked[r, :, :], ALU.mult))
    for k in range(1, E1):
        step(v.tensor_tensor(total[r, :, :, k], total[r, :, :, k], total[r, :, :, k - 1], ALU.add))
    step(v.tensor_tensor(total[r, 0, :, :], total[r, 0, :, :], per_k, ALU.mult))
    step(v.tensor_scalar(total[r, 1, :, :], total[r, 1, :, :], -1.0, 1.0, ALU.mult, ALU.add))
    step(v.tensor_tensor(total[r, 1, :, :], total[r, 1, :, :], per_k, ALU.mult))
    step(v.tensor_tensor(root[r, :, :], total[r, 0, :, :], total[r, 0, :, :], ALU.mult))
    step(v.tensor_tensor(root[r, :, :], root[r, :, :], total[r, 1, :, :], ALU.add))
    step(v.tensor_scalar(root[r, :, :], root[r, :, :], 0.0, None, ALU.max))
    take_root()
    step(v.tensor_tensor(total[r, 0, :, :], total[r, 0, :, :], root[r, :, :], ALU.subtract))
    step(v.tensor_tensor(cut[r, :, :], ranked[r, :, :], total[r, 0, :, :], ALU.is_ge))
    step(v.scalar_tensor_tensor(cut[r, :, :], total[r, 0, :, :], 1.0, cut[r, :, :], ALU.add, ALU.mult))
    step(v.tensor_reduce(tau[r, :], cut[r, :, :], AX.X, ALU.max))
    step(v.tensor_scalar(tau[r, :], tau[r, :], -1.0, None, ALU.add))
    over(logit[r, :, :])
    step(v.tensor_tensor(ranked[r, :, :], cut[r, :, :], cut[r, :, :], ALU.mult))
    step(v.tensor_reduce(mass[r, :], ranked[r, :, :], AX.X, ALU.add))
    step(v.tensor_reduce(slope[r, :], cut[r, :, :], AX.X, ALU.add))
    step(v.reciprocal(slope[r, :], slope[r, :]))
    step(v.tensor_scalar(mass[r, :], mass[r, :], -1.0, 0.5, ALU.add, ALU.mult))
    step(v.tensor_tensor(mass[r, :], mass[r, :], slope[r, :], ALU.mult))
    step(v.tensor_tensor(tau[r, :], tau[r, :], mass[r, :], ALU.add))
    over(logit[r, :, :])
    step(v.tensor_tensor(ranked[r, :, :], cut[r, :, :], cut[r, :, :], ALU.mult))
    step(v.tensor_reduce(mass[r, :], ranked[r, :, :], AX.X, ALU.add))
    step(v.reciprocal(mass[r, :], mass[r, :]))
    step(v.tensor_tensor(cut[r, :, :], ranked[r, :, :], wide(mass), ALU.mult))
    step(v.scalar_tensor_tensor(gate[r, :, :], cut[r, :, :], THRESH, cut[r, :, :], ALU.is_gt, ALU.mult))


def stage_gated(nc, io, H, mv, rstd, out):
    with Stage(nc, "gm") as st:
        sb, ps, sem = st.sb, st.ps, st.sem
        xh, xl = sb("xh", [P, DK, B * S], R32), sb("xl", [P, DK, B * S], R32)
        logit, root = sb("logit", [P, TILES, E1]), sb("root", [P, TILES, E1])
        raw1, raw2 = sb("raw1", [P, DK, F1]), sb("raw2", [P, FT, D])
        w1h, w1l = sb("w1h", [P, DK, F1], R32), sb("w1l", [P, DK, F1], R32)
        w2h, w2l = sb("w2h", [P, FT, D], R32), sb("w2l", [P, FT, D], R32)
        b1, b2 = sb("b1", [P, E1, FT]), sb("b2", [P, E1, D])
        gate = sb("gate", [P, TILES, E1])
        hid = [sb(f"hid{i}", [P, CHUNK]) for i in range(2)]
        hh, hl = sb("hh", [P, FT, CHUNK], R32), sb("hl", [P, FT, CHUNK], R32)
        b_loaded, raw1_loaded, raw2_loaded = sem("b_loaded"), sem("raw1_loaded"), sem("raw2_loaded")
        w1_split, w2_split, chain, prepared = sem("w1_split"), sem("w2_split"), sem("chain"), sem("prepared")
        root_ready, root_taken = sem("root_ready"), sem("root_taken")
        up_mm, relued, halved, split, down_mm, added, biased, stored, paused = (
            sem(n) for n in ("up_mm", "relued", "halved", "split", "down_mm", "added", "biased", "stored", "paused"))
        BANKS, HIDS, DOWNS = 4, 2, CTILES

        def load(sp, e):
            since(sp, w1_split, e * 2)
            sp.dma_start(raw1[:, :, :], io["gm_w1"][ds(e, 1), :, :].rearrange("o (k p) f -> p (o k) f", p=P)).then_inc(raw1_loaded, 16)
            since(sp, w2_split, e * 2)
            sp.dma_start(raw2[:, :, :], io["gm_w2"][ds(e, 1), :, :].rearrange("o (k p) f -> p (o k) f", p=P)).then_inc(raw2_loaded, 16)

        def first_split(pool):
            for raw, high, low, got, done in ((raw1, w1h, w1l, raw1_loaded, w1_split), (raw2, w2h, w2l, raw2_loaded, w2_split)):
                pool.wait_ge(got, 16)
                split_high(nc.gpsimd, high[:, :, :], raw[:, :, :]).then_inc(done, 1)
                pool.wait_ge(done, 1)
                split_low(nc.gpsimd, low[:, :, :], raw[:, :, :], high[:, :, :]).then_inc(done, 1)

        stage_gates(nc, io, H, mv, rstd, xh, xl, logit, lambda sp: load(sp, 0), first_split)
        up = [ps(f"up{i}", [P, 512]) for i in range(4)]
        down = [ps(f"down{i}", [P, 512]) for i in range(CTILES)]

        def experts(eng, body, prepare=lambda e: None, between=lambda e: None):
            with eng.Fori(0, E1 - 1) as e:
                prepare(e)
                with eng.Fori(0, NCHUNK) as j:
                    body(e, j, e * NCHUNK + j)
                between(e + 1)
            prepare(E1 - 1)
            with eng.Fori(0, NCHUNK) as j:
                body(E1 - 1, j, (E1 - 1) * NCHUNK + j)

        with nc.Block() as block:

            @block.sync
            def _(sp):
                sp.dma_start(b1[:, :, :], io["gm_b1"].rearrange("p (e f) -> p e f", e=E1)).then_inc(b_loaded, 16)
                sp.dma_start(b2[:, :, :].rearrange("p e d -> p (e d)"), io["gm_b2"].broadcast_to([P, E1 * D])).then_inc(b_loaded, 16)

                with sp.Fori(1, E1) as e:
                    load(sp, e)
                out_v = out.rearrange("b (t p) d -> p (b t) d", p=ROWS)
                for j in range(NCHUNK):
                    sp.wait_ge(added, BANKS + ((E1 - 1) * NCHUNK + j + 1) * CTILES)
                    tiles = slice(j * CTILES, (j + 1) * CTILES)
                    sp.dma_start(out_v[:, tiles, :], H[0:ROWS, tiles, :]).then_inc(stored, 16)
                sp.wait_ge(stored, 16 * NCHUNK)

            @block.gpsimd
            def _(pool):
                with pool.Fori(1, E1) as e:
                    for raw, high, low, done in ((raw1, w1h, w1l, w1_split), (raw2, w2h, w2l, w2_split)):
                        pool.wait_ge(done, e * 2 + 1)
                        split_low(nc.gpsimd, low[:, :, :], raw[:, :, :], high[:, :, :]).then_inc(done, 1)

            @block.vector
            def _(dve):
                dve.sem_inc(split, HIDS)
                dve.sem_inc(added, BANKS)

                def take_root():
                    dve.sem_inc(root_ready, 1)
                    dve.wait_ge(root_taken, 1)

                entmax(nc, dve, st, chain, root, take_root, logit, gate)
                dve.wait_ge(b_loaded, 32)

                def body(e, j, c):
                    for f in range(FT):
                        k = c * FT + f
                        dve.wait_ge(relued, k + 1 + BANKS)
                        if f == 0:
                            dve.wait_ge(down_mm, c * CTILES + DOWNS)
                        split_high(nc.vector, hh[:, f, :], hid[f % 2][:, :]).then_inc(halved, 1)
                        dve.wait_ge(halved, k + 1)
                        split_low(nc.vector, hl[:, f, :], hid[f % 2][:, :], hh[:, f, :]).then_inc(split, 1)
                    for t in range(CTILES):
                        tile = j * CTILES + t
                        row = H[0:ROWS, ds(tile, 1), :].rearrange("p a d -> p (a d)")
                        g = gate[0:ROWS, ds(tile, 1), ds(e, 1)].rearrange("p a e -> p (a e)")
                        nc.vector.scalar_tensor_tensor(row, b2[0:ROWS, ds(e, 1), :].rearrange("p a d -> p (a d)"), g, row, ALU.mult, ALU.add).then_inc(biased, 1)
                    for t in range(CTILES):
                        tile = j * CTILES + t
                        row = H[0:ROWS, ds(tile, 1), :].rearrange("p a d -> p (a d)")
                        g = gate[0:ROWS, ds(tile, 1), ds(e, 1)].rearrange("p a e -> p (a e)")
                        dve.wait_ge(biased, c * CTILES + t + 1)
                        dve.wait_ge(down_mm, c * CTILES + t + 1 + DOWNS)
                        nc.vector.scalar_tensor_tensor(row, down[t][0:ROWS, 0:D], g, row, ALU.mult, ALU.add).then_inc(added, 1)

                experts(dve, body)

            @block.scalar
            def _(act):
                act.wait_ge(root_ready, 1)
                nc.scalar.activation(root[0:ROWS, :, :], root[0:ROWS, :, :], ACT.Sqrt).then_inc(root_taken, 1)
                act.sem_inc(relued, BANKS)
                act.wait_ge(b_loaded, 32)

                def body(e, j, c):
                    for f in range(FT):
                        k = c * FT + f
                        act.wait_ge(up_mm, k + 1)
                        act.wait_ge(split, k + 1)
                        nc.scalar.activation(hid[f % 2][:, :], up[f % 4][:, 0:CHUNK], ACT.Relu,
                                             bias=b1[:, ds(e, 1), f:f + 1].rearrange("p a f -> p (a f)")).then_inc(relued, 1)

                def between(e):
                    act.wait_ge(raw1_loaded, e * 16 + 16)
                    act.wait_ge(up_mm, e * NCHUNK * FT)
                    nc.scalar.activation(w1h[:, :, :], raw1[:, :, :], ACT.Copy).then_inc(w1_split, 1)
                    act.wait_ge(raw2_loaded, e * 16 + 16)
                    act.wait_ge(down_mm, DOWNS + e * NCHUNK * CTILES)
                    nc.scalar.activation(w2h[:, :, :], raw2[:, :, :], ACT.Copy).then_inc(w2_split, 1)

                experts(act, body, between=between)

            @block.tensor
            def _(pe):
                pe.sem_inc(down_mm, DOWNS)

                def prepare(e):
                    pause(pe, w1_split, e * 2 + 2, prepared)

                def body(e, j, c):
                    tok = ds(j * CHUNK, CHUNK)
                    for f in range(FT):
                        k = c * FT + f
                        pe.wait_ge(relued, k + 1)
                        cols = slice(f * P, (f + 1) * P)
                        terms = [(w, x, kk) for kk in range(DK) for w, x in three((w1h, w1l), (xh, xl))]
                        for i, (w, x, kk) in enumerate(terms):
                            last = nc.tensor.matmul(up[f % 4][:, 0:CHUNK], w[:, kk, cols], x[:, kk, tok], start=(i == 0), stop=(i == len(terms) - 1))
                        last.then_inc(up_mm, 1)
                    pe.wait_ge(w2_split, e * 2 + 2)
                    for t in range(CTILES):
                        rows = slice(t * ROWS, (t + 1) * ROWS)
                        pe.wait_ge(added, c * CTILES + t + 1)
                        for f in range(FT):
                            if t == 0:
                                pe.wait_ge(split, c * FT + f + 1 + HIDS)
                            for i, (h, w) in enumerate(three((hh, hl), (w2h, w2l))):
                                last = nc.tensor.matmul(down[t][0:ROWS, 0:D], h[:, f, rows], w[:, f, :], start=(f == 0 and i == 0), stop=(f == FT - 1 and i == 2))
                        last.then_inc(down_mm, 1)

                experts(pe, body, prepare)


def build(nc, io, out, upto=9):
    with ExitStack() as ctx:
        H = ctx.enter_context(nc.sbuf_tensor("H", [P, TILES, D], F32))
        mv = ctx.enter_context(nc.sbuf_tensor("mv", [P, TILES, 2], F32))
        rstd = ctx.enter_context(nc.sbuf_tensor("rstd", [P, TILES], F32))
        stage_tokens(nc, io, H, mv)
        stage_rstd(nc, "r0", mv, rstd)
        if upto >= 1:
            stage_attention(nc, io, H, mv, rstd)
            stage_rstd(nc, "r1", mv, rstd)
        if upto >= 2:
            stage_routed(nc, io, H, mv, rstd)
            stage_rstd(nc, "r2", mv, rstd)
        if upto >= 3:
            stage_features(nc, io, H, mv, rstd)
            stage_rstd(nc, "r3", mv, rstd)
        if upto >= 4:
            stage_gated(nc, io, H, mv, rstd, out)
        if upto < 4:
            with nc.semaphore("stored") as stored, nc.Block() as block:

                @block.sync
                def _(sp):
                    sp.dma_start(out.rearrange("b (t p) d -> p (b t) d", p=ROWS), H[0:ROWS, :, :]).then_inc(stored, 16)
                    sp.wait_ge(stored, 16)


def layout(i):
    a = {k: np.asarray(v) for k, v in i.items()}
    zeros = lambda *s: np.zeros(s, np.float32)
    io = {}
    io["xt"] = a["x"].reshape(B * S, PATCH).T
    io["tok_in"] = np.concatenate([
        np.concatenate([a["L0_tok_W_h"].T, a["L0_tok_b_h"][None], zeros(1, HID)], 0),
        np.concatenate([a["L0_tok_W_r"].T, a["L0_tok_b_r"][None], a["L0_tok_b_o"][None]], 0)], 1)
    io["tok_out"] = a["L0_tok_W_o"].T
    io["ident"] = np.eye(P, dtype=np.float32)
    for k in "qkvo":
        io[f"at_w{k}"] = a[f"L0_attn_W{k}"]
    for k in "qk":
        io[f"at_b{k}"] = a[f"L0_attn_b{k}"].reshape(G, P).T
    for k in "vo":
        io[f"at_b{k}"] = a[f"L0_attn_b{k}"][None]
    rel = np.concatenate([a["L0_attn_rel_key"], zeros(P, HD)], 0)
    first = RANGE - 1 - (S - 2)
    io["at_relx"] = np.concatenate([rel[first - r:first - r + RELN].T for r in range(XR)], 0)
    p = np.arange(P)
    r, j = np.arange(BLK)[:, None], np.arange(MINW)[None]
    tri = np.concatenate([np.where(j > r + late, MASKED, 0.0) for late in (0, BLK)], 1)
    io["at_cst"] = np.concatenate([
        p[:, None] // HD == np.arange(GH), p[:, None] // HD == np.arange(BLK) % XR,
        np.pad(r == p % BLK, ((0, P - BLK), (0, 0))), np.pad(tri, ((0, P - BLK), (0, 0)))], 1).astype(np.float32)
    io["rt_wr"], io["rt_br"] = a["L0_ffn_router_w"].T, a["L0_ffn_router_b"][None]
    io["rt_ids"] = np.arange(E0, dtype=np.float32)[None]
    io["rt_own"] = np.pad(np.repeat(np.eye(E0, dtype=np.float32), H0, 1), ((0, P - E0), (0, 0)))
    io["rt_w1"] = a["L0_ffn_weights1"].transpose(1, 0, 2).reshape(D, E0 * H0)
    io["rt_w2"] = a["L0_ffn_weights2"].reshape(E0 * H0, D)
    io["rt_b1"] = a["L0_ffn_bias1"].reshape(PR, P).T
    io["rt_b2"] = np.concatenate([a["L0_ffn_bias2"], zeros(P - E0, D)], 0)
    w, bias = a["L1_attn_W_attn"], a["L1_attn_b_attn"]
    io["fe_w"], io["fe_wo"] = w, a["L1_attn_W_proj"]
    io["fe_bias"] = bias[:2 * D].reshape(2 * G, P).T
    io["fe_bv"], io["fe_bo"] = bias[None, 2 * D:], a["L1_attn_b_proj"][None]
    om = zeros(2, QH, HD, QH, M)
    for h in range(QH):
        om[0, h, :, h, :] = a["L1_attn_omega"]
        om[1, h, :, h, :] = -0.5
    io["fe_omega"] = om.reshape(P, QH * M)
    s_, t_ = np.arange(ROWS)[:, None], np.arange(S)[None]
    io["fe_causal"] = np.concatenate([s_ <= t_, s_ <= t_[:, :ROWS]], 1).astype(np.float32)
    io["ga_wr"], io["ga_br"] = a["L1_ffn_Wr"], a["L1_ffn_br"][None]
    io["gm_w1"], io["gm_w2"] = a["L1_ffn_W1"], a["L1_ffn_W2"]
    io["gm_b1"] = a["L1_ffn_b1"].reshape(E1 * FT, P).T
    io["gm_b2"] = a["L1_ffn_b2"].reshape(1, E1 * D)
    return {k: np.ascontiguousarray(v) for k, v in io.items()}


UPTO = 9


def kernel(**inputs):
    import concourse.bacc as bacc
    from concourse.bass_utils import run_bass_kernel_spmd

    nc = bacc.Bacc("TRN2", target_bir_lowering=False, num_devices=1)
    arrays = layout(inputs)
    io = {k: nc.dram_tensor(f"in_{k}", v.shape, mybir.dt.from_np(v.dtype), kind="ExternalInput").ap() for k, v in arrays.items()}
    out = nc.dram_tensor("out", (B, S, D), F32, kind="ExternalOutput").ap()
    build(nc, io, out, UPTO)
    r = run_bass_kernel_spmd(nc, [{f"in_{k}": v for k, v in arrays.items()}], core_ids=[0])
    return r.results[0]["out"]
```

```python
from contextlib import ExitStack

import numpy as np

import concourse.bass as bass
from concourse import mybir
from concourse.alu_op_type import AluOpType as ALU

F32 = mybir.dt.float32
BF16 = mybir.dt.bfloat16
U32 = mybir.dt.uint32
R32 = mybir.dt.float32r
ACT = mybir.ActivationFunctionType
AX = mybir.AxisListType

B, S, D = 16, 250, 256
PATCH = 16
ROWS = S // 2
TILES = 2 * B
P = 128
DK = D // P
HEADS, HD = 16, 16
GH = P // HD
G = HEADS // GH
HID = 512
NHID = HID // P
XCAT = 2 * PATCH + 2
LN_EPS = 1e-5
MASKED = -1.0e30


def ds(start, size):
    return bass.ds(start, size)


def since(eng, sem, value):
    if not isinstance(value, int) or value > 0:
        eng.wait_ge(sem, value)


def pause(eng, sem, value, paused):
    eng.wait_ge(sem, value)
    eng.sem_inc(paused, 1)




def split_high(eng, high, x):
    return eng.tensor_copy(high, x)


def split_low(eng, low, x, high):
    return eng.tensor_tensor(low, x, high.bitcast(F32), ALU.subtract)


def three(high_low_a, high_low_b):
    (ah, al), (bh, bl) = high_low_a, high_low_b
    return (ah, bh), (ah, bl), (al, bh)


class Stage:

    def __init__(self, nc, name):
        self.nc, self.name, self.ctx = nc, name, ExitStack()

    def __enter__(self):
        return self

    def __exit__(self, *a):
        return self.ctx.__exit__(*a)

    def sb(self, name, shape, dt=F32):
        return self.ctx.enter_context(self.nc.sbuf_tensor(f"{self.name}_{name}", shape, dt))

    def ps(self, name, shape, dt=F32):
        return self.ctx.enter_context(self.nc.psum_tensor(f"{self.name}_{name}", shape, dt))

    def sem(self, name):
        return self.ctx.enter_context(self.nc.semaphore(f"{self.name}_{name}"))


class RowStats:

    def __init__(self, nc, st, H, mv):
        self.nc, self.H, self.mv = nc, H, mv
        self.halves, self.moments = st.sb("halves", [P, 2, 6]), st.sb("moments", [P, 2, 2])
        self.halves_done, self.moments_done = st.sem("halves_done"), st.sem("moments_done")
        self.mv_done, self.paused = st.sem("mv_done"), st.sem("paused")

    def take(self, dve, n, written, count):
        v, rows = self.nc.vector, slice(0, ROWS)
        pause(dve, written, count, self.paused)
        for t in range(2):
            v.bn_stats(self.halves[rows, t, :], self.H[rows, ds(n * 2 + t, 1), :].rearrange("p a d -> p (a d)")).then_inc(self.halves_done, 1)
        pause(dve, self.halves_done, n * 2 + 2, self.paused)
        if not (isinstance(n, int) and n == 0):
            pause(dve, self.mv_done, n, self.paused)
        for t in range(2):
            v.bn_aggr(self.moments[rows, t, :], self.halves[rows, t, :]).then_inc(self.moments_done, 1)
        dve.wait_ge(self.moments_done, n * 2 + 2)
        v.tensor_copy(self.mv[rows, ds(n * 2, 2), :], self.moments[rows, :, :]).then_inc(self.mv_done, 1)


def stage_rstd(nc, name, mv, rstd):
    with Stage(nc, name) as st:
        veps = st.sb("veps", [P, TILES])
        root = st.sb("root", [P, TILES])
        eps_added, rooted, done = st.sem("eps_added"), st.sem("rooted"), st.sem("done")
        with nc.Block() as block:

            @block.vector
            def _(dve):
                nc.vector.tensor_scalar(veps[0:ROWS, :], mv[0:ROWS, :, 1], LN_EPS, None, ALU.add).then_inc(eps_added, 1)
                dve.wait_ge(rooted, 1)
                nc.vector.reciprocal(rstd[0:ROWS, :], root[0:ROWS, :]).then_inc(done, 1)

            @block.scalar
            def _(act):
                act.wait_ge(eps_added, 1)
                nc.scalar.activation(root[0:ROWS, :], veps[0:ROWS, :], ACT.Sqrt).then_inc(rooted, 1)


def sequences(eng, body):
    body(0, 0)
    body(0, 1)
    with eng.Fori(1, B // 2) as it:
        body(it, 0)
        body(it, 1)


def stage_tokens(nc, io, H, mv, preload, preclear):
    with Stage(nc, "tok") as st:
        win = st.sb("win", [P, HID + D])
        wout = st.sb("wout", [P, NHID, D])
        xcat = [st.sb(f"xcat{s}", [P, S]) for s in range(2)]
        wouth, woutl = st.sb("wouth", [P, NHID, D], R32), st.sb("woutl", [P, NHID, D], R32)
        hid = [st.sb(f"hid{s}", [P, NHID, S]) for s in range(2)]
        hh, hl = ([st.sb(f"hid{part}{s}", [P, NHID, S], R32) for s in range(2)] for part in ("high", "low"))
        stats = RowStats(nc, st, H, mv)
        hid_ps = [st.ps(f"hid_ps{s}", [P, 2, 512]) for s in range(2)]
        out_ps = [st.ps(f"out_ps{s}", [P, 2, 512]) for s in range(2)]
        w_loaded, cleared = st.sem("w_loaded"), st.sem("cleared")
        x_loaded = [st.sem(f"x_loaded{s}") for s in range(2)]
        hid_mm, hid_act, out_mm = st.sem("hid_mm"), st.sem("hid_act"), st.sem("out_mm")
        h_done, w_split, halved, split = (st.sem(n) for n in ("h_done", "w_split", "halved", "split"))
        x_used = st.sem("x_used")

        def one_ahead(eng, ahead, behind):
            ahead(0, 0)
            ahead(1, 1)
            behind(0, 0)
            with eng.Fori(1, B // 2) as it:
                ahead(it * 2, 0)
                behind(it * 2 - 1, 1)
                ahead(it * 2 + 1, 1)
                behind(it * 2, 0)
            behind(B - 1, 1)

        with nc.Block() as block:

            @block.sync
            def _(sp):
                sp.wait_ge(cleared, 1)
                sp.dma_start(win[0:XCAT, :], io["tok_in"][:, :]).then_inc(w_loaded, 16)
                sp.dma_start(wout[:, :, :], io["tok_out"].rearrange("(k p) d -> p k d", p=P)).then_inc(w_loaded, 16)
                sp.wait_ge(cleared, 5)

                def load(it, s):
                    n = it * 2 + s
                    since(sp, x_used, n - 1)
                    sp.dma_start(xcat[s][0:PATCH, :], io["xt"][:, ds(n * S, S)]).then_inc(x_loaded[s], 16)

                load(0, 0)
                load(0, 1)
                preload(sp)
                with sp.Fori(1, B // 2) as it:
                    load(it, 0)
                    load(it, 1)

            @block.gpsimd
            def _(pool):
                preclear()

            @block.vector
            def _(dve):
                nc.vector.memset(win[:, :], 0.0).then_inc(cleared, 1)
                for s in range(2):
                    nc.vector.memset(xcat[s][:, :], 0.0).then_inc(cleared, 1)
                    dve.wait_ge(cleared, 2 * s + 2)
                    nc.vector.memset(xcat[s][0:XCAT, :], 1.0).then_inc(cleared, 1)

                def parts(n, s):
                    for half in range(2):
                        k, f = n * 2 + half, slice(2 * half, 2 * half + 2)
                        dve.wait_ge(hid_act, k + 1)
                        since(dve, out_mm, n - 1)
                        split_high(nc.vector, hh[s][:, f, :], hid[s][:, f, :]).then_inc(halved, 1)
                        dve.wait_ge(halved, k + 1)
                        split_low(nc.vector, hl[s][:, f, :], hid[s][:, f, :], hh[s][:, f, :]).then_inc(split, 1)

                dve.wait_ge(w_loaded, 32)
                split_high(nc.vector, wouth[:, :, :], wout[:, :, :]).then_inc(w_split, 1)
                dve.wait_ge(w_split, 1)
                split_low(nc.vector, woutl[:, :, :], wout[:, :, :], wouth[:, :, :]).then_inc(w_split, 1)

                def take(n, s):
                    dve.wait_ge(out_mm, n + 1)
                    nc.vector.tensor_copy(H[0:ROWS, ds(n * 2, 2), :], out_ps[s][0:ROWS, :, 0:D]).then_inc(h_done, 1)
                    stats.take(dve, n, h_done, n + 1)

                one_ahead(dve, parts, take)

            @block.scalar
            def _(act):
                def silu(it, s):
                    n = it * 2 + s
                    for half in range(2):
                        act.wait_ge(hid_mm, n * 2 + half + 1)
                        since(act, split, (n - 1) * 2)
                        nc.scalar.activation(hid[s][:, 2 * half:2 * half + 2, :], hid_ps[s][:, half, 0:2 * S].rearrange("p (a t) -> p a t", a=2), ACT.Silu).then_inc(hid_act, 1)

                sequences(act, silu)

            @block.tensor
            def _(pe):
                pe.wait_ge(w_loaded, 32)

                def hidden(n, s):
                    pe.wait_ge(x_loaded[s], n * 8 + 16 - 8 * s)
                    for half in range(2):
                        since(pe, hid_act, n * 2 + half - 3)
                        for k in range(2):
                            f = 2 * half + k
                            last = nc.tensor.matmul(hid_ps[s][:, half, k * S:(k + 1) * S], win[:, f * P:(f + 1) * P], xcat[s][:, :], start=True, stop=True)
                        last.then_inc(hid_mm, 1)
                    since(pe, h_done, n - 1)
                    for t in range(2):
                        last = nc.tensor.matmul(out_ps[s][0:ROWS, t, 0:D], xcat[s][:, t * ROWS:(t + 1) * ROWS], win[:, HID:HID + D], start=True, stop=False)
                    last.then_inc(x_used, 1)

                def output(n, s):
                    if isinstance(n, int) and n == 0:
                        pe.wait_ge(w_split, 2)
                    pe.wait_ge(split, n * 2 + 2)
                    for t in range(2):
                        tok = slice(t * ROWS, (t + 1) * ROWS)
                        terms = [(h, w, f) for f in range(NHID) for h, w in three((hh[s], hl[s]), (wouth, woutl))]
                        for i, (h, w, f) in enumerate(terms):
                            last = nc.tensor.matmul(out_ps[s][0:ROWS, t, 0:D], h[:, f, tok], w[:, f, :], start=False, stop=(i == len(terms) - 1))
                    last.then_inc(out_mm, 1)

                one_ahead(pe, hidden, output)


QP = 256
BLK = 16
NBLK = QP // BLK
PAIRS = NBLK // 2
XR = P // HD
MINW = 112
RELN = S - 2 + MINW
RANGE = 512


def pair_width(c):
    return min(max(32 * (c + 1), MINW), S)


def stage_attention(nc, io, H, mv, rstd, ident):
    with Stage(nc, "at") as st:
        sb, ps, sem = st.sb, st.ps, st.sem
        Q, K, V, O = range(4)
        wh, wl = sb("wh", [P, DK, 4, D], R32), sb("wl", [P, DK, 4, D], R32)
        bq, bk = sb("bq", [P, G]), sb("bk", [P, G])
        bv, bo = sb("bv", [P, D]), sb("bo", [P, D])
        relx = sb("relx", [P, RELN])
        cst = sb("cst", [P, GH + BLK + P + 2 * MINW])
        headmask, rowmask = cst[:, 0:GH], cst[:, GH:GH + BLK]
        msel, tri = sb("msel", [P, P], BF16), sb("tri", [P, 2, MINW], BF16)
        qT = [sb(f"qT{s}", [P, G, QP]) for s in range(2)]
        vpad = [sb(f"vpad{s}", [P, 2, G, GH * (P + HD)]) for s in range(2)]
        qrow = [sb(f"qrow{g}", [P, NBLK, 2, GH, BLK]) for g in range(G)]
        prob = [sb(f"prob{c}", [P, 2, P if c < PAIRS // 2 else 2 * P]) for c in range(PAIRS)]
        qd = nc.dram_tensor("q_rows", (B, G, P, QP), F32).ap()

        loaded, w_loaded, w_split = sem("loaded"), sem("w_loaded"), sem("w_split")
        cleared, consts, x_low, a_low = sem("cleared"), sem("consts"), sem("x_low"), sem("a_low")
        xn_done, xt_mm, xt_evac = sem("xn_done"), sem("xt_mm"), sem("xt_evac")
        q_mm, k_mm, v_mm = sem("q_mm"), sem("k_mm"), sem("v_mm")
        q_evac, k_evac, v_evac = sem("q_evac"), sem("k_evac"), sem("v_evac")
        q_stored, qrep_loaded, spread = sem("q_stored"), sem("qrep_loaded"), sem("spread")
        scored, maxed, exped = sem("scored"), sem("maxed"), sem("exped")
        summed, normed = sem("summed"), sem("normed")
        turned_mm, turned_evac = sem("turned_mm"), sem("turned_evac")
        pv_mm, a_evac = sem("pv_mm"), sem("a_evac")
        wo_mm, wo_evac, h_done = sem("wo_mm"), sem("wo_evac"), sem("h_done")

        def preload(sp):
            sp.dma_start(ident[:, :], io["ident"]).then_inc(loaded, 16)
            for n, k in ((Q, "at_wq"), (K, "at_wk"), (V, "at_wv"), (O, "at_wo")):
                sp.dma_start(w[:, :, n, :], io[k].rearrange("(k p) d -> p k d", p=P)).then_inc(w_loaded, 16)
            for t, k in ((bq, "at_bq"), (bk, "at_bk"), (relx, "at_relx"), (cst, "at_cst")):
                sp.dma_start(t[:, :], io[k]).then_inc(loaded, 16)
            sp.dma_start(bv[:, :], io["at_bv"].broadcast_to([P, D])).then_inc(loaded, 16)
            sp.dma_start(bo[:, :], io["at_bo"].broadcast_to([P, D])).then_inc(loaded, 16)

        def preclear():
            for v in vpad:
                nc.gpsimd.memset(v[:, :, :, :], 0.0).then_inc(cleared, 1)
            for t in qrow:
                nc.gpsimd.memset(t[:, :, :, :, :], 0.0).then_inc(cleared, 1)
            for t in prob:
                nc.gpsimd.memset(t[:, :, :], 0.0).then_inc(cleared, 1)
            for t in qT:
                nc.gpsimd.memset(t[:, :, :], 0.0).then_inc(cleared, 1)
            nc.gpsimd.wait_ge(w_loaded, 16 * 4)
            split_high(nc.gpsimd, wh[:, :, :, :], w[:, :, :, :]).then_inc(w_split, 1)
            nc.gpsimd.wait_ge(w_split, 1)
            split_low(nc.gpsimd, wl[:, :, :, :], w[:, :, :, :], wh[:, :, :, :]).then_inc(w_split, 1)

        with Stage(nc, "aw") as weights:
            w = weights.sb("w", [P, DK, 4, D])
            stage_tokens(nc, io, H, mv, preload, preclear)
        stage_rstd(nc, "r0", mv, rstd)
        xn, xh, xl = sb("xn", [P, 2, D]), sb("xh", [P, DK, S], R32), sb("xl", [P, DK, S], R32)
        kT = [sb(f"kT{s}", [P, G, S]) for s in range(2)]
        qrep = sb("qrep", [P, GH, QP])
        qdiag = [sb(f"qdiag{g}", [P, NBLK, GH, BLK]) for g in range(G)]
        pT = [sb(f"pT{g}", [P, 3, NBLK // 2, P]) for g in range(G)]
        ah, al = sb("ah", [P, G, QP], R32), sb("al", [P, G, QP], R32)
        nmax, total, rtotal = sb("nmax", [P, 4, 2]), sb("total", [P, 4, 2]), sb("rtotal", [P, 4, 2])
        proj, stats = sb("proj", [P, 2, D]), RowStats(nc, st, H, mv)
        score = [ps(f"score{i}", [P, 2, QP]) for i in range(4)]
        turned = [ps(f"turned{i}", [P, 2, 2, P]) for i in range(2)]
        F = [ps(f"front{i}", [P, 512]) for i in range(2)]

        def side(g, c):
            return {(0, 4): "pv", (0, 6): "wo", (1, 1): "xt", (1, 2): "q", (1, 3): "k", (1, 4): "pv", (1, 6): "v"}.get((g, c))

        def schedule(it, s, first, last):
            n = it * 2 + s
            for g in range(G):
                for c in range(PAIRS):
                    step = side(g, c)
                    if first and g == 0:
                        step = None
                    if last and step in ("xt", "q", "k", "v"):
                        step = None
                    yield g, c, n * 16 + g * PAIRS + c, step

        def run(eng, start, body, finish):
            start()
            body(0, 0, True, False)
            body(0, 1, False, False)
            with eng.Fori(1, B // 2 - 1) as it:
                body(it, 0, False, False)
                body(it, 1, False, False)
            body(B // 2 - 1, 0, False, False)
            body(B // 2 - 1, 1, False, True)
            finish()

        with nc.Block() as block:

            @block.sync
            def _(sp):
                def copies(it, s):
                    n = it * 2 + s
                    sp.wait_ge(q_evac, n + 1)
                    sp.dma_start(qd[ds(n, 1), :, :, :].rearrange("o g p i -> p (o g) i"), qT[s][:, :, :]).then_inc(q_stored, 16)
                    sp.wait_ge(q_stored, n * 16 + 16)
                    for g in range(G):
                        since(sp, spread, (n * 2 + g) * 3)
                        for r in range(XR):
                            sp.dma_start(qrep[r * HD:(r + 1) * HD, :, :],
                                         qd[ds(n, 1), g, :, :].rearrange("o (h d) i -> d (o h) i", d=HD)).then_inc(qrep_loaded, 16)

                sequences(sp, copies)

            @block.gpsimd
            def _(pool):
                pool.wait_ge(loaded, 16 * 7)

                def spreads(it, s):
                    n = it * 2 + s
                    for g in range(G):
                        u = n * 2 + g
                        pool.wait_ge(q_evac, n + 1)
                        since(pool, scored, (u - 1) * PAIRS)
                        nc.gpsimd.tensor_tensor(
                            qdiag[g][:, :, :, :],
                            qT[s][:, g, :].rearrange("p (a r) -> p a r", r=BLK).unsqueeze(2).broadcast_to([P, NBLK, GH, BLK]),
                            headmask.unsqueeze(1).unsqueeze(3).broadcast_to([P, NBLK, GH, BLK]), ALU.mult).then_inc(spread, 1)
                        pool.wait_ge(qrep_loaded, (n * 2 + g + 1) * 16 * XR)
                        for kt in range(2):
                            nc.gpsimd.tensor_tensor(
                                qrow[g][:, :, kt, :, kt * XR:(kt + 1) * XR],
                                qrep[:, :, :].rearrange("p h (a k r) -> p k a h r", k=2, r=XR)[:, kt, :, :, :],
                                rowmask[:, kt * XR:(kt + 1) * XR].unsqueeze(1).unsqueeze(1).broadcast_to([P, NBLK, GH, XR]), ALU.mult).then_inc(spread, 1)

                pool.wait_ge(cleared, 4 + PAIRS + 2)
                sequences(pool, spreads)

            @block.vector
            def _(dve):
                def normalise(m):
                    since(dve, xt_mm, m)
                    for t in range(2):
                        nc.vector.tensor_scalar(xn[0:ROWS, t, :], H[0:ROWS, ds(m * 2 + t, 1), :].rearrange("p a d -> p (a d)"),
                                                mv[0:ROWS, ds(m * 2 + t, 1), 0:1].rearrange("p a o -> p (a o)"), rstd[0:ROWS, ds(m * 2 + t, 1)],
                                                ALU.subtract, ALU.mult).then_inc(xn_done, 1)

                def low_x(m):
                    dve.wait_ge(xt_evac, m + 1)
                    since(dve, v_mm, m)
                    split_low(nc.vector, xl[:, :, :], F[1][:, 0:DK * S].rearrange("p (k t) -> p k t", k=DK), xh[:, :, :]).then_inc(x_low, 1)

                def low_a(g, m):
                    dve.wait_ge(a_evac, m * 2 + g + 1)
                    since(dve, wo_mm, m)
                    split_low(nc.vector, al[:, g, :], F[g][:, 0:QP], ah[:, g, :]).then_inc(a_low, 1)

                def k_out(s, m):
                    dve.wait_ge(k_mm, m + 1)
                    since(dve, scored, (m - 1) * G * PAIRS)
                    nc.vector.tensor_tensor(kT[s][:, :, :], F[1][:, 0:G * S].rearrange("p (g t) -> p g t", g=G),
                                            bk[:, :].unsqueeze(2).broadcast_to([P, G, S]), ALU.add).then_inc(k_evac, 1)

                def v_out(s, m):
                    dve.wait_ge(v_mm, m + 1)
                    since(dve, pv_mm, m * 2 - 2)
                    for jt, rows in ((0, P), (1, S - P)):
                        for g in range(G):
                            dst = vpad[s][0:rows, jt, g, :].rearrange("p (h c) -> p h c", h=GH)[:, :, 0:HD]
                            nc.vector.tensor_tensor(dst, F[0][0:rows, jt * D + g * P:jt * D + (g + 1) * P].rearrange("p (h c) -> p h c", h=GH),
                                                    bv[0:rows, g * P:(g + 1) * P].rearrange("p (h c) -> p h c", h=GH), ALU.add).then_inc(v_evac, 1)

                def wo_out(m):
                    dve.wait_ge(wo_mm, m + 1)
                    nc.vector.tensor_tensor(proj[0:ROWS, :, :], F[0][0:ROWS, :].rearrange("p (t d) -> p t d", t=2),
                                            bo[0:ROWS, :].unsqueeze(1).broadcast_to([ROWS, 2, D]), ALU.add).then_inc(wo_evac, 1)
                    dve.wait_ge(wo_evac, m + 1)
                    rows = H[0:ROWS, ds(m * 2, 2), :]
                    nc.vector.tensor_tensor(rows, rows, proj[0:ROWS, :, :], ALU.add).then_inc(h_done, 1)
                    stats.take(dve, m, h_done, m + 1)

                def norm(k, g, c):
                    i, w = c % 4, pair_width(c)
                    dve.wait_ge(exped, k * 2 + 2)
                    nc.vector.reciprocal(rtotal[:, i, :], total[:, i, :]).then_inc(summed, 1)
                    dve.wait_ge(summed, k + 1)
                    for a in range(2):
                        nc.vector.tensor_scalar(prob[c][:, a, 0:w], prob[c][:, a, 0:w], rtotal[:, i, a:a + 1], None, ALU.mult).then_inc(normed, 1)

                def start():
                    dve.wait_ge(loaded, 16 * 7)
                    nc.vector.tensor_copy(msel[:, :], cst[:, GH + BLK:GH + BLK + P]).then_inc(consts, 1)
                    nc.vector.tensor_copy(tri[:, :, :], cst[:, GH + BLK + P:GH + BLK + P + 2 * MINW].rearrange("p (a j) -> p a j", a=2)).then_inc(consts, 1)
                    nc.vector.tensor_scalar(bq[:, :], bq[:, :], HD ** -0.5, None, ALU.mult).then_inc(consts, 1)
                    normalise(0)
                    low_x(0)
                    k_out(0, 0)
                    v_out(0, 0)

                def body(it, s, first, last):
                    n = it * 2 + s
                    for g, c, k, step in schedule(it, s, first, last):
                        if g == 0 and c == 0 and not last:
                            normalise(n + 1)
                        if g == 0 and c == 5 and not first:
                            low_a(1, n - 1)
                        if g == 1 and c == 5:
                            low_a(0, n)
                        if g == 1 and c == 2 and not last:
                            low_x(n + 1)
                        dve.wait_ge(scored, k + 1)
                        nc.vector.tensor_reduce(nmax[:, c % 4, :], score[c % 4][:, :, 0:pair_width(c)], AX.X, ALU.max, negate=True).then_inc(maxed, 1)
                        if not (first and g == 0 and c == 0):
                            norm(k - 1, g, (c - 1) % PAIRS)
                        if step == "k":
                            k_out(1 - s, n + 1)
                        if step == "v":
                            v_out(1 - s, n + 1)
                        if step == "wo":
                            wo_out(n - 1)

                def finish():
                    norm(B * 16 - 1, 1, PAIRS - 1)
                    low_a(1, B - 1)
                    wo_out(B - 1)

                run(dve, start, body, finish)

            @block.scalar
            def _(act):
                def xt_out(m):
                    act.wait_ge(xt_mm, m + 1)
                    since(act, v_mm, m)
                    nc.scalar.activation(xh[:, :, :], F[1][:, 0:DK * S].rearrange("p (k t) -> p k t", k=DK), ACT.Copy).then_inc(xt_evac, 1)

                def q_out(s, m):
                    act.wait_ge(q_mm, m + 1)
                    since(act, spread, (m - 1) * 6)
                    since(act, q_stored, (m - 1) * 16)
                    for g in range(G):
                        last = nc.scalar.activation(qT[s][:, g, 0:S], F[0][:, g * S:(g + 1) * S], ACT.Identity, bias=bq[:, g:g + 1], scale=HD ** -0.5)
                    last.then_inc(q_evac, 1)

                def a_out(g, m):
                    act.wait_ge(pv_mm, m * 2 + g + 1)
                    since(act, wo_mm, m)
                    nc.scalar.activation(ah[:, g, :], F[g][:, 0:QP], ACT.Copy).then_inc(a_evac, 1)

                def turned_out(k, u, g, c):
                    act.wait_ge(turned_mm, k + 1)
                    if c == 0:
                        since(act, pv_mm, u - 1)
                    if c < PAIRS // 2:
                        nc.scalar.activation(pT[g][:, 0:1, 2 * c:2 * c + 2, :], turned[c % 2][:, 0:1, :, :], ACT.Copy).then_inc(turned_evac, 1)
                    else:
                        a = 2 * c - NBLK // 2
                        nc.scalar.activation(pT[g][:, 1:3, a:a + 2, :], turned[c % 2][:, :, :, :], ACT.Copy).then_inc(turned_evac, 1)

                def start():
                    act.wait_ge(consts, 3)
                    act.wait_ge(cleared, 4 + PAIRS + 2)
                    xt_out(0)
                    q_out(0, 0)

                def body(it, s, first, last):
                    n = it * 2 + s
                    for g, c, k, step in schedule(it, s, first, last):
                        i, w = c % 4, pair_width(c)
                        act.wait_ge(maxed, k + 1)
                        since(act, turned_mm, k - PAIRS + 1)
                        for a in range(2):
                            nc.scalar.activation(prob[c][:, a, 0:w], score[i][:, a, 0:w], ACT.Exp, bias=nmax[:, i, a:a + 1],
                                                 accum_out=total[:, i, a:a + 1]).then_inc(exped, 1)
                        if not (first and g == 0 and c < 2):
                            turned_out(k - 2, n * 2 + g - (c < 2), (g if c >= 2 else 1 - g), (c - 2) % PAIRS)
                        if step == "xt":
                            xt_out(n + 1)
                        if step == "q":
                            q_out(1 - s, n + 1)
                        if step == "pv":
                            if g == 0:
                                a_out(1, n - 1)
                            else:
                                a_out(0, n)

                def finish():
                    last = B * 16
                    turned_out(last - 2, 2 * B - 1, 1, PAIRS - 2)
                    turned_out(last - 1, 2 * B - 1, 1, PAIRS - 1)
                    a_out(1, B - 1)

                run(act, start, body, finish)

            @block.tensor
            def _(pe):
                def project(out, operands):
                    terms = [ab for lhs, rhs in operands for ab in three(lhs, rhs)]
                    for i, (a, b) in enumerate(terms):
                        last = nc.tensor.matmul(out, a, b, start=(i == 0), stop=(i == len(terms) - 1))
                    return last

                def xt_in(m):
                    pe.wait_ge(xn_done, m * 2 + 2)
                    since(pe, a_low, m * 2 - 2)
                    for k in range(DK):
                        for t in range(2):
                            last = nc.tensor.transpose(F[1][:, k * S + t * ROWS:k * S + (t + 1) * ROWS], xn[0:ROWS, t, k * P:(k + 1) * P], ident[0:ROWS, 0:ROWS])
                    last.then_inc(xt_mm, 1)

                def q_in(m):
                    pe.wait_ge(x_low, m + 1)
                    if isinstance(m, int) and m == 1:
                        pe.wait_ge(v_evac, 4)
                    since(pe, wo_evac, m - 1)
                    for g in range(G):
                        last = project(F[0][:, g * S:(g + 1) * S], [((wh[:, k, Q, g * P:(g + 1) * P], wl[:, k, Q, g * P:(g + 1) * P]), (xh[:, k, :], xl[:, k, :])) for k in range(DK)])
                    last.then_inc(q_mm, 1)

                def k_in(m):
                    pe.wait_ge(x_low, m + 1)
                    for g in range(G):
                        last = project(F[1][:, g * S:(g + 1) * S], [((wh[:, k, K, g * P:(g + 1) * P], wl[:, k, K, g * P:(g + 1) * P]), (xh[:, k, :], xl[:, k, :])) for k in range(DK)])
                    last.then_inc(k_mm, 1)

                def v_in(m):
                    if isinstance(m, int) and m == 0:
                        pe.wait_ge(q_evac, 1)
                    else:
                        pe.wait_ge(a_low, m * 2 - 1)
                    for jt, rows in ((0, P), (1, S - P)):
                        tok = slice(jt * P, jt * P + rows)
                        last = project(F[0][0:rows, jt * D:(jt + 1) * D], [((xh[:, k, tok], xl[:, k, tok]), (wh[:, k, V, :], wl[:, k, V, :])) for k in range(DK)])
                    last.then_inc(v_mm, 1)

                def pv_in(s, g, m):
                    bank, u = F[g], m * 2 + g
                    pe.wait_ge(turned_evac, (u + 1) * PAIRS)
                    pe.wait_ge(v_evac, m * 4 + 4)
                    if isinstance(m, int) and m == B - 1:
                        pe.wait_ge(wo_evac, B - 1) if g == 0 else pe.wait_ge(k_evac, B)
                    elif g == 1:
                        pe.wait_ge(k_evac, m + 2)
                    else:
                        pe.wait_ge(q_evac, m + 2)
                    for h in range(GH):
                        for jt in range(2):
                            rhs = pT[g][:, 0:2, :, h * BLK:(h + 1) * BLK].rearrange("p b a r -> p (b a) r") if jt == 0 else pT[g][:, 2, :, h * BLK:(h + 1) * BLK]
                            last = nc.tensor.matmul(bank[:, jt * P:QP], vpad[s][:, jt, g, h * P:(h + 1) * P], rhs, start=(h == 0 and jt == 0), stop=(h == GH - 1 and jt == 1))
                    last.then_inc(pv_mm, 1)

                def wo_in(m):
                    pe.wait_ge(a_low, m * 2 + 2)
                    if not (isinstance(m, int) and m == B - 1):
                        pe.wait_ge(v_evac, m * 4 + 8)
                    for t in range(2):
                        tok = slice(t * ROWS, (t + 1) * ROWS)
                        last = project(F[0][0:ROWS, t * D:(t + 1) * D], [((ah[:, g, tok], al[:, g, tok]), (wh[:, g, O, :], wl[:, g, O, :])) for g in range(G)])
                    last.then_inc(wo_mm, 1)

                def scores(s, g, c, k, n):
                    if c == 0:
                        pe.wait_ge(spread, (n * 2 + g + 1) * 3)
                        if g == 0:
                            pe.wait_ge(k_evac, n + 1)
                    since(pe, exped, 2 * k - 6)
                    w = pair_width(c)
                    for a in range(2):
                        blk = 2 * c + a
                        out = score[c % 4][:, a, 0:w]
                        nc.tensor.matmul(out, qdiag[g][:, blk, :, :].rearrange("p h r -> p (h r)"), kT[s][:, g, 0:w], start=True, stop=False)
                        for kt in range(2):
                            off = S - 2 - BLK * blk - XR * kt
                            nc.tensor.matmul(out, qrow[g][:, blk, kt, :, :].rearrange("p h r -> p (h r)"), relx[:, off:off + w], start=False, stop=False)
                        last = nc.tensor.matmul(score[c % 4][:, a, 32 * c:w], msel[:, :], tri[:, a, 0:w - 32 * c], start=False, stop=True)
                    last.then_inc(scored, 1)

                def turn(g, c, k):
                    pe.wait_ge(normed, 2 * k + 2)
                    since(pe, turned_evac, k - 1)
                    for jt in range(1 if c < PAIRS // 2 else 2):
                        for a in range(2):
                            last = nc.tensor.transpose(turned[c % 2][:, jt, a, :], prob[c][:, a, jt * P:(jt + 1) * P], ident[:, :])
                    last.then_inc(turned_mm, 1)

                def start():
                    pe.wait_ge(loaded, 16 * 7)
                    xt_in(0)
                    q_in(0)
                    k_in(0)
                    pe.wait_ge(consts, 3)
                    v_in(0)

                def body(it, s, first, last):
                    n = it * 2 + s
                    for g, c, k, step in schedule(it, s, first, last):
                        scores(s, g, c, k, n)
                        if not (first and g == 0 and c < 2):
                            turn(g if c >= 2 else 1 - g, (c - 2) % PAIRS, k - 2)
                        if step == "xt":
                            xt_in(n + 1)
                        if step == "q":
                            q_in(n + 1)
                        if step == "k":
                            k_in(n + 1)
                        if step == "v":
                            v_in(n + 1)
                        if step == "pv" and g == 0:
                            pv_in(1 - s, 1, n - 1)
                        if step == "pv" and g == 1:
                            pv_in(s, 0, n)
                        if step == "wo":
                            wo_in(n - 1)

                def finish():
                    last = B * 16
                    turn(1, PAIRS - 2, last - 2)
                    turn(1, PAIRS - 1, last - 1)
                    pv_in(1, 1, B - 1)
                    wo_in(B - 1)

                run(pe, start, body, finish)


CHUNK = 2 * S
CTILES = CHUNK // ROWS
NCHUNK = B * S // CHUNK
E0, H0 = 32, 64
PR = E0 * H0 // P


def normalise_rows(nc, H, mv, rstd, dst, tile):
    return nc.vector.tensor_scalar(dst, H[0:ROWS, ds(tile, 1), :].rearrange("p a d -> p (a d)"),
                                   mv[0:ROWS, ds(tile, 1), 0:1].rearrange("p a o -> p (a o)"), rstd[0:ROWS, ds(tile, 1)],
                                   ALU.subtract, ALU.mult)


def chunk_loop(eng, body):
    body(0, 0, False)
    body(0, 1, False)
    with eng.Fori(1, NCHUNK // 2 - 1) as it:
        body(it, 0, False)
        body(it, 1, False)
    body(NCHUNK // 2 - 1, 0, False)
    body(NCHUNK // 2 - 1, 1, True)


def stage_routed(nc, io, H, mv, rstd, ident):
    with Stage(nc, "rt") as st:
        sb, ps, sem = st.sb, st.ps, st.sem
        w1h, w1l = sb("w1h", [P, DK, E0 * H0], R32), sb("w1l", [P, DK, E0 * H0], R32)
        w2h, w2l = sb("w2h", [P, PR, D], R32), sb("w2l", [P, PR, D], R32)
        b1, b2 = sb("b1", [P, PR]), sb("b2", [P, D])
        wr, br, ids = sb("wr", [P, DK, E0]), sb("br", [P, E0]), sb("ids", [P, E0])
        own = sb("own", [P, PR, P], BF16)
        xn = sb("xn", [P, CTILES, D])
        xt = [sb(f"xt{s}", [P, DK, CHUNK]) for s in range(2)]
        xh, xl = ([sb(f"x{part}{s}", [P, DK, CHUNK], R32) for s in range(2)] for part in ("high", "low"))
        hid = [sb(f"hid{i}", [P, CHUNK]) for i in range(2)]
        logit, top, topid = sb("logit", [P, CTILES, E0]), sb("top", [P, CTILES, 8]), sb("topid", [P, CTILES, 8], U32)
        topf, onehot = sb("topf", [P, CTILES, 8]), sb("onehot", [P, CTILES, E0])
        onehotT = [sb(f"onehotT{s}", [P, CHUNK]) for s in range(2)]
        push = [sb(f"push{s}", [P, CHUNK], BF16) for s in range(2)]
        stats = RowStats(nc, st, H, mv)
        up = [ps(f"up{i}", [P, 512]) for i in range(2)]
        down = [ps(f"down{i}", [P, 2, D]) for i in range(2)]
        xt_ps, logit_ps, hot_ps = ps("xt_ps", [P, DK, 512]), ps("logit_ps", [P, CTILES, E0 * 4]), ps("hot_ps", [P, 512])
        loaded, cleared, own_made = sem("loaded"), sem("cleared"), sem("own_made")
        own_loaded = sem("own_loaded")
        w1_loaded, w2_loaded, w1_split, w2_split = sem("w1_loaded"), sem("w2_loaded"), sem("w1_split"), sem("w2_split")
        x_high, x_low, halved, split = sem("x_high"), sem("x_low"), sem("halved"), sem("split")
        xn_done, xt_mm, xt_evac, logit_mm, route, hot_mm, hot_evac, push_made = (
            sem(n) for n in ("xn_done", "xt_mm", "xt_evac", "logit_mm", "route", "hot_mm", "hot_evac", "push_made"))
        up_mm, relued, down_mm, h_done, paused = (sem(n) for n in ("up_mm", "relued", "down_mm", "h_done", "picked"))
        STEPS = 1 + 2 * CTILES + 2

        dve, act, pe = nc.vector, nc.scalar, nc.tensor

        def normalise(j, tiles=range(CTILES)):
            if 0 in tiles:
                since(dve, xt_mm, j)
            for t in tiles:
                normalise_rows(nc, H, mv, rstd, xn[0:ROWS, t, :], j * CTILES + t).then_inc(xn_done, 1)

        def choose(s, j):
            dve.wait_ge(logit_mm, j + 1)
            since(dve, hot_mm, j)
            nc.vector.tensor_tensor(logit[0:ROWS, :, :], logit_ps[0:ROWS, :, 0:E0], br[0:ROWS, :].unsqueeze(1).broadcast_to([ROWS, CTILES, E0]), ALU.add).then_inc(route, 1)
            pause(dve, route, j * STEPS + 1, paused)
            for t in range(CTILES):
                nc.vector.max(top[0:ROWS, t, :], logit[0:ROWS, t, :]).then_inc(route, 1)
            pause(dve, route, j * STEPS + 1 + CTILES, paused)
            for t in range(CTILES):
                nc.vector.max_index(topid[0:ROWS, t, :], top[0:ROWS, t, :], logit[0:ROWS, t, :]).then_inc(route, 1)
            dve.wait_ge(route, j * STEPS + 1 + 2 * CTILES)
            nc.vector.tensor_copy(topf[0:ROWS, :, :], topid[0:ROWS, :, :]).then_inc(route, 1)
            dve.wait_ge(route, j * STEPS + 2 + 2 * CTILES)
            nc.vector.tensor_tensor(onehot[0:ROWS, :, :], ids[0:ROWS, :].unsqueeze(1).broadcast_to([ROWS, CTILES, E0]),
                                    topf[0:ROWS, :, 0:1].broadcast_to([ROWS, CTILES, E0]), ALU.is_equal).then_inc(route, 1)

        def pushes(s, j):
            dve.wait_ge(hot_evac, j + 1)
            nc.vector.tensor_scalar(push[s][0:E0, :], onehotT[s][0:E0, :], -1.0, -MASKED, ALU.add, ALU.mult).then_inc(push_made, 1)

        def add(j):
            for half in range(2):
                dve.wait_ge(down_mm, j * 2 + half + 1)
                rows = H[0:ROWS, ds(j * CTILES + 2 * half, 2), :]
                nc.vector.scalar_tensor_tensor(rows, down[half][0:ROWS, :, :], 0.0, rows, ALU.max, ALU.add).then_inc(h_done, 1)
                stats.take(dve, j * 2 + half, h_done, j * 2 + half + 1)

        def low_x(s, j):
            dve.wait_ge(x_high, j + 1)
            since(dve, up_mm, (j - 1) * PR)
            split_low(nc.vector, xl[s][:, :, :], xt[s][:, :, :], xh[s][:, :, :]).then_inc(x_low, 1)

        def low_weights(low, high, raw, high_done):
            flat = lambda t: t[:, :, :].rearrange("p a b -> p (a b)")
            dve.wait_ge(high_done, 1)
            split_low(nc.vector, flat(low), raw[:, :], flat(high)).then_inc(high_done, 1)

        def xt_out(s, j):
            act.wait_ge(xt_mm, j + 1)
            since(act, x_low, j - 1)
            nc.scalar.activation(xt[s][:, :, :], xt_ps[:, :, 0:CHUNK], ACT.Copy).then_inc(xt_evac, 1)

        def high_x(s, j):
            since(act, up_mm, (j - 1) * PR)
            act.wait_ge(xt_evac, j + 1)
            nc.scalar.activation(xh[s][:, :, :], xt[s][:, :, :], ACT.Copy).then_inc(x_high, 1)

        def hot_out(s, j):
            act.wait_ge(hot_mm, j + 1)
            nc.scalar.activation(onehotT[s][0:E0, :], hot_ps[0:E0, 0:CHUNK], ACT.Copy).then_inc(hot_evac, 1)

        def xt_in(j):
            pe.wait_ge(xn_done, (j + 1) * CTILES)
            for k in range(DK):
                for t in range(CTILES):
                    last = nc.tensor.transpose(xt_ps[:, k, t * ROWS:(t + 1) * ROWS], xn[0:ROWS, t, k * P:(k + 1) * P], ident[0:ROWS, 0:ROWS])
            last.then_inc(xt_mm, 1)

        def logits_in(s, j):
            pe.wait_ge(xt_evac, j + 1)
            since(pe, route, (j - 1) * STEPS + 1)
            for t in range(CTILES):
                for k in range(DK):
                    last = nc.tensor.matmul(logit_ps[0:ROWS, t, 0:E0], xt[s][:, k, t * ROWS:(t + 1) * ROWS], wr[:, k, :], start=(k == 0), stop=(k == DK - 1))
            last.then_inc(logit_mm, 1)

        def hot_in(j):
            pe.wait_ge(route, (j + 1) * STEPS)
            since(pe, hot_evac, j)
            for t in range(CTILES):
                last = nc.tensor.transpose(hot_ps[0:E0, t * ROWS:(t + 1) * ROWS], onehot[0:ROWS, t, :], ident[0:ROWS, 0:ROWS])
            last.then_inc(hot_mm, 1)

        with Stage(nc, "rw") as weights:
            raw1, raw2 = weights.sb("raw1", [P, DK * E0 * H0]), weights.sb("raw2", [P, PR * D])
            raw_own = weights.sb("raw_own", [P, PR * P])
            with nc.Block() as block:

                @block.sync
                def _(sp):
                    sp.dma_start(wr[:, :, :], io["rt_wr"].rearrange("(k p) e -> p k e", p=P)).then_inc(loaded, 16)
                    for t, k in ((br, "rt_br"), (ids, "rt_ids")):
                        sp.dma_start(t[:, :], io[k].broadcast_to([P, E0])).then_inc(loaded, 16)
                    sp.dma_start(raw_own[0:E0, :], io["rt_own"]).then_inc(own_loaded, 16)
                    sp.dma_start(raw1[:, :].rearrange("p (k e) -> p k e", k=DK), io["rt_w1"].rearrange("(k p) e -> p k e", p=P)).then_inc(w1_loaded, 16)
                    sp.dma_start(raw2[:, :].rearrange("p (k e) -> p k e", k=PR), io["rt_w2"].rearrange("(k p) e -> p k e", p=P)).then_inc(w2_loaded, 16)
                    for t, k in ((b1, "rt_b1"), (b2, "rt_b2")):
                        sp.dma_start(t[:, :], io[k]).then_inc(own_loaded, 16)

                @block.gpsimd
                def _(pool):
                    for s in range(2):
                        nc.gpsimd.memset(onehotT[s][:, :], 0.0).then_inc(cleared, 1)
                        nc.gpsimd.memset(push[s][:, :], 0.0).then_inc(cleared, 1)
                    nc.gpsimd.memset(own[:, :, :], 0.0).then_inc(cleared, 1)

                @block.vector
                def _(dve):
                    normalise(0)
                    dve.wait_ge(loaded, 16 * 3)
                    choose(0, 0)
                    low_x(0, 0)
                    low_weights(w1l, w1h, raw1, w1_split)
                    dve.wait_ge(cleared, 5)
                    pushes(0, 0)
                    dve.wait_ge(own_loaded, 16 * 3)
                    nc.vector.tensor_copy(own[0:E0, :, :].rearrange("p a b -> p (a b)"), raw_own[0:E0, :]).then_inc(own_made, 1)
                    low_weights(w2l, w2h, raw2, w2_split)

                @block.scalar
                def _(act):
                    flat = lambda t: t[:, :, :].rearrange("p a b -> p (a b)")
                    xt_out(0, 0)
                    high_x(0, 0)
                    act.wait_ge(w1_loaded, 16)
                    nc.scalar.activation(flat(w1h), raw1[:, :], ACT.Copy).then_inc(w1_split, 1)
                    act.wait_ge(cleared, 4)
                    hot_out(0, 0)
                    act.wait_ge(w2_loaded, 16)
                    nc.scalar.activation(flat(w2h), raw2[:, :], ACT.Copy).then_inc(w2_split, 1)

                @block.tensor
                def _(pe):
                    xt_in(0)
                    pe.wait_ge(loaded, 16 * 3)
                    logits_in(0, 0)
                    hot_in(0)

        hh, hl = sb("hh", [P, PR, CHUNK], R32), sb("hl", [P, PR, CHUNK], R32)
        with nc.Block() as block:

            @block.vector
            def _(dve):
                def parts(j, pr):
                    k = j * PR + pr
                    dve.wait_ge(relued, k + 1)
                    if pr == 0:
                        since(dve, down_mm, j * 2)
                    split_high(nc.vector, hh[:, pr, :], hid[pr % 2][:, :]).then_inc(halved, 1)
                    dve.wait_ge(halved, k + 1)
                    split_low(nc.vector, hl[:, pr, :], hid[pr % 2][:, :], hh[:, pr, :]).then_inc(split, 1)

                def body(it, s, last):
                    j = it * 2 + s
                    for pr in range(PR):
                        parts(j, pr)
                        if not last and 1 <= pr < 1 + CTILES:
                            normalise(j + 1, (pr - 1,))
                    if not last:
                        choose(1 - s, j + 1)
                        low_x(1 - s, j + 1)
                        pushes(1 - s, j + 1)
                    add(j)

                chunk_loop(dve, body)

            @block.scalar
            def _(act):
                def body(it, s, last):
                    j = it * 2 + s
                    for pr in range(PR):
                        act.wait_ge(up_mm, j * PR + pr + 1)
                        since(act, split, j * PR + pr - 1)
                        nc.scalar.activation(hid[pr % 2][:, :], up[pr % 2][:, 0:CHUNK], ACT.Relu, bias=b1[:, pr:pr + 1]).then_inc(relued, 1)
                        if pr == 6 and not last:
                            xt_out(1 - s, j + 1)
                        if pr == 8 and not last:
                            high_x(1 - s, j + 1)
                    if not last:
                        hot_out(1 - s, j + 1)

                chunk_loop(act, body)

            @block.tensor
            def _(pe):
                def body(it, s, last_chunk):
                    j = it * 2 + s
                    pe.wait_ge(push_made, j + 1)
                    pe.wait_ge(x_low, j + 1)
                    for pr in range(PR):
                        since(pe, relued, j * PR + pr - 1)
                        for k in range(DK):
                            for i, (w, x) in enumerate(three((w1h, w1l), (xh[s], xl[s]))):
                                nc.tensor.matmul(up[pr % 2][:, 0:CHUNK], w[:, k, pr * P:(pr + 1) * P], x[:, k, :], start=(k == 0 and i == 0), stop=False)
                        nc.tensor.matmul(up[pr % 2][:, 0:CHUNK], own[:, pr, :], push[s][:, :], start=False, stop=True).then_inc(up_mm, 1)
                        if not last_chunk:
                            if pr == 6:
                                xt_in(j + 1)
                            if pr == 9:
                                logits_in(1 - s, j + 1)
                    if isinstance(j, int) and j == 0:
                        pe.wait_ge(w2_split, 2)
                    pe.wait_ge(hot_evac, j + 1)
                    for t in range(CTILES):
                        tok = slice(t * ROWS, (t + 1) * ROWS)
                        out = down[t // 2][0:ROWS, t % 2, :]
                        if t % 2 == 0:
                            since(pe, h_done, j * 2 - 1 + t // 2)
                        nc.tensor.matmul(out, onehotT[s][:, tok], b2[:, :], start=True, stop=False)
                        for pr in range(PR):
                            if t == 0:
                                pe.wait_ge(split, j * PR + pr + 1)
                            for i, (h, w) in enumerate(three((hh, hl), (w2h, w2l))):
                                last = nc.tensor.matmul(out, h[:, pr, tok], w[:, pr, :], start=False, stop=(pr == PR - 1 and i == 2))
                        if t % 2 == 1:
                            last.then_inc(down_mm, 1)
                        if t == 1 and not last_chunk:
                            hot_in(j + 1)

                chunk_loop(pe, body)


QH = 4
NQ = HEADS // QH
HP = QH * HD
M = P
DEN_EPS = 1e-6


def stage_features(nc, io, H, mv, rstd, ident):
    with Stage(nc, "fe") as st:
        sb, ps, sem = st.sb, st.ps, st.sem
        Q, K, V, O = range(4)
        w, wh, wl = sb("w", [P, DK, 4, D]), sb("wh", [P, DK, 4, D], R32), sb("wl", [P, DK, 4, D], R32)
        bias, bias4 = sb("bias", [P, 2, G]), sb("bias4", [P, 2, G])
        bv, bo = sb("bv", [P, D]), sb("bo", [P, D])
        omega, causal = sb("omega", [P, QH, M]), sb("causal", [P, S + ROWS])
        xn, xh, xl = sb("xn", [P, 2, D]), sb("xh", [P, DK, S], R32), sb("xl", [P, DK, S], R32)
        omega_h, omega_l = sb("omega_h", [P, QH, M], R32), sb("omega_l", [P, QH, M], R32)
        z = sb("z", [P, 2, NQ, S])
        zh, zl = ([sb(f"z{part}{s}", [P, 2, NQ, S], R32) for s in range(2)] for part in ("high", "low"))
        vone = [sb(f"vone{s}", [P, 2, NQ, QH * (P + HD)]) for s in range(2)]
        phi = [sb(f"phi{i}", [P, 2, S]) for i in range(2)]
        att = [sb(f"att{i}", [P, S + ROWS]) for i in range(2)]
        den, yT = sb("den", [P, S]), [sb(f"yT{s}", [P, G, S]) for s in range(2)]
        yh, yl = sb("yh", [P, G, S], R32), sb("yl", [P, G, S], R32)
        proj, stats = sb("proj", [P, 2, D]), RowStats(nc, st, H, mv)
        F = [ps(f"front{i}", [P, 512]) for i in range(2)]
        phi_ps = [ps(f"phi_ps{i}", [P, 512]) for i in range(2)]
        att_ps = [ps(f"att_ps{i}", [P, 512]) for i in range(2)]
        av_ps = [ps(f"av_ps{i}", [P, 512]) for i in range(2)]
        qkv_loaded, loaded, cleared, consts = sem("qkv_loaded"), sem("loaded"), sem("cleared"), sem("consts")
        xn_done, xt_mm, xt_evac = sem("xn_done"), sem("xt_mm"), sem("xt_evac")
        q_mm, k_mm, v_mm, lin_out, sq_out, v_evac = (sem(n) for n in ("q_mm", "k_mm", "v_mm", "lin_out", "sq_out", "v_evac"))
        w_split, x_low, y_split, paused = sem("w_split"), sem("x_low"), sem("y_split"), sem("y_paused")
        wo_split = sem("wo_split")
        z_high, z_low = sem("z_high"), sem("z_low")
        phi_mm, exped, att_mm, masked, av_mm = (sem(n) for n in ("phi_mm", "exped", "att_mm", "masked", "av_mm"))
        divided, proj_mm, proj_evac, h_done = (sem(n) for n in ("divided", "proj_mm", "proj_evac", "h_done"))
        LIN = 4

        SIDE = {7: "xt", 9: "q", 12: "k", 14: "v"}

        def run(eng, start, body, finish):
            start()
            body(0, 0, True, False)
            body(0, 1, False, False)
            with eng.Fori(1, B // 2 - 1) as it:
                body(it, 0, False, False)
                body(it, 1, False, False)
            body(B // 2 - 1, 0, False, False)
            body(B // 2 - 1, 1, False, True)
            finish()

        with nc.Block() as block:

            @block.sync
            def _(sp):
                sp.dma_start(w[:, :, Q:O, :], io["fe_w"].rearrange("(k p) (n d) -> p k n d", p=P, n=3)).then_inc(qkv_loaded, 16)
                sp.dma_start(w[:, :, O, :], io["fe_wo"].rearrange("(k p) d -> p k d", p=P)).then_inc(loaded, 16)
                sp.dma_start(bias[:, :, :], io["fe_bias"].rearrange("p (c g) -> p c g", c=2)).then_inc(loaded, 16)
                sp.dma_start(omega[:, :, :], io["fe_omega"].rearrange("p (h m) -> p h m", h=QH)).then_inc(loaded, 16)
                sp.dma_start(causal[0:ROWS, :], io["fe_causal"]).then_inc(loaded, 16)
                sp.dma_start(bv[:, :], io["fe_bv"].broadcast_to([P, D])).then_inc(loaded, 16)
                sp.dma_start(bo[:, :], io["fe_bo"].broadcast_to([P, D])).then_inc(loaded, 16)

            @block.gpsimd
            def _(pool):
                for s in range(2):
                    nc.gpsimd.memset(vone[s][:, :, :, :], 0.0).then_inc(cleared, 1)
                pool.wait_ge(cleared, 2)
                for s in range(2):
                    for t in range(2):
                        for qt in range(NQ):
                            ones = vone[s][:, t, qt, :].rearrange("p (h c) -> p h c", h=QH)[:, :, HP:HP + HD]
                            nc.gpsimd.memset(ones, 1.0).then_inc(cleared, 1)

                def low_z(s, m, which):
                    pool.wait_ge(z_high, m * 2 + which + 1)
                    since(pool, phi_mm, (m - 1) * HEADS)
                    split_low(nc.gpsimd, zl[s][:, which, :, :], z[:, which, :, :], zh[s][:, which, :, :]).then_inc(z_low, 1)

                def split_y(s, m, g):
                    pause(pool, divided, (m * NQ + 2 * g + 2) * 3, paused)
                    if not isinstance(m, int) or m > 0:
                        pause(pool, proj_mm, m, paused)
                    split_high(nc.gpsimd, yh[:, g, :], yT[s][:, g, :]).then_inc(y_split, 1)
                    pool.wait_ge(y_split, m * 4 + 2 * g + 1)
                    split_low(nc.gpsimd, yl[:, g, :], yT[s][:, g, :], yh[:, g, :]).then_inc(y_split, 1)

                def start():
                    pool.wait_ge(loaded, 16 * 6)
                    split_high(nc.gpsimd, wh[:, :, O, :], w[:, :, O, :]).then_inc(wo_split, 1)
                    low_z(0, 0, 0)
                    low_z(0, 0, 1)
                    pool.wait_ge(wo_split, 1)
                    split_low(nc.gpsimd, wl[:, :, O, :], w[:, :, O, :], wh[:, :, O, :]).then_inc(wo_split, 1)

                def body(it, s, first, last):
                    n = it * 2 + s
                    if not first:
                        split_y(1 - s, n - 1, 1)
                    if not last:
                        low_z(1 - s, n + 1, 0)
                    split_y(s, n, 0)
                    if not last:
                        low_z(1 - s, n + 1, 1)

                run(pool, start, body, lambda: split_y(1, B - 1, 1))

            @block.vector
            def _(dve):
                def normalise(m):
                    since(dve, xt_mm, m)
                    for t in range(2):
                        normalise_rows(nc, H, mv, rstd, xn[0:ROWS, t, :], m * 2 + t).then_inc(xn_done, 1)

                def low_x(m):
                    dve.wait_ge(xt_evac, m + 1)
                    since(dve, v_mm, m)
                    split_low(nc.vector, xl[:, :, :], F[1][:, 0:DK * S].rearrange("p (k t) -> p k t", k=DK), xh[:, :, :]).then_inc(x_low, 1)

                def linear(s, m, which, mm):
                    dve.wait_ge(mm, m + 1)
                    dve.wait_ge(sq_out, m * 2 * LIN + (which + 1) * LIN)
                    since(dve, z_low, (m - 1) * 2 + which + 1)
                    for g in range(G):
                        for half in range(2):
                            src = slice(half * HP, (half + 1) * HP)
                            nc.vector.tensor_scalar(z[0:HP, which, 2 * g + half, :], F[which][src, g * S:(g + 1) * S],
                                                    bias[src, which, g:g + 1], HD ** -0.5, ALU.add, ALU.mult).then_inc(lin_out, 1)

                def v_out(s, m):
                    dve.wait_ge(v_mm, m + 1)
                    since(dve, av_mm, (m - 1) * HEADS)
                    for qt in range(NQ):
                        nc.vector.tensor_tensor(vone[s][0:ROWS, :, qt, :].rearrange("p t (h c) -> p t h c", h=QH)[:, :, :, 0:HD],
                                                F[0][0:ROWS, :].rearrange("p (t q h d) -> p q t h d", t=2, q=NQ, h=QH)[:, qt, :, :, :],
                                                bv[0:ROWS, qt * HP:(qt + 1) * HP].rearrange("p (h d) -> p h d", h=QH).unsqueeze(1).broadcast_to([ROWS, 2, QH, HD]),
                                                ALU.add).then_inc(v_evac, 1)

                def denominators(m, qt):
                    dve.wait_ge(av_mm, (m * NQ + qt + 1) * QH)
                    since(dve, divided, (m * NQ + qt) * 3)
                    nc.vector.tensor_scalar(den[0:HP, :], av_ps[qt % 2][HP:P, 0:S], DEN_EPS * M, None, ALU.add).then_inc(divided, 1)

                def invert(m, qt):
                    dve.wait_ge(divided, (m * NQ + qt) * 3 + 1)
                    nc.vector.reciprocal(den[0:HP, :], den[0:HP, :]).then_inc(divided, 1)

                def quotient(s, m, qt):
                    dve.wait_ge(divided, (m * NQ + qt) * 3 + 2)
                    since(dve, y_split, (m - 1) * 4)
                    half = (qt % 2) * HP
                    nc.vector.tensor_tensor(yT[s][half:half + HP, qt // 2, :], av_ps[qt % 2][0:HP, 0:S], den[0:HP, :], ALU.mult).then_inc(divided, 1)

                def proj_out(m):
                    dve.wait_ge(proj_mm, m + 1)
                    nc.vector.tensor_tensor(proj[0:ROWS, :, :], F[1][0:ROWS, :].rearrange("p (t d) -> p t d", t=2), bo[0:ROWS, :].unsqueeze(1).broadcast_to([ROWS, 2, D]), ALU.add).then_inc(proj_evac, 1)
                    dve.wait_ge(proj_evac, m + 1)
                    rows = H[0:ROWS, ds(m * 2, 2), :]
                    nc.vector.tensor_tensor(rows, rows, proj[0:ROWS, :, :], ALU.add).then_inc(h_done, 1)

                def mask(k, h):
                    dve.wait_ge(att_mm, k + 1)
                    since(dve, av_mm, k - 1)
                    nc.vector.tensor_tensor(att[h % 2][0:ROWS, :], att_ps[h % 2][0:ROWS, 0:S + ROWS], causal[0:ROWS, :], ALU.mult).then_inc(masked, 1)

                def start():
                    normalise(0)
                    dve.wait_ge(qkv_loaded, 16)
                    for n in (Q, K, V):
                        split_high(nc.vector, wh[:, :, n, :], w[:, :, n, :]).then_inc(w_split, 1)
                        dve.wait_ge(w_split, 2 * n + 1)
                        split_low(nc.vector, wl[:, :, n, :], w[:, :, n, :], wh[:, :, n, :]).then_inc(w_split, 1)
                        if n == Q:
                            low_x(0)
                    dve.wait_ge(loaded, 16 * 6)
                    nc.vector.tensor_scalar(bias4[:, :, :], bias[:, :, :], HD ** -0.5, None, ALU.mult).then_inc(consts, 1)
                    split_high(nc.vector, omega_h[:, :, :], omega[:, :, :]).then_inc(consts, 1)
                    dve.wait_ge(consts, 2)
                    split_low(nc.vector, omega_l[:, :, :], omega[:, :, :], omega_h[:, :, :]).then_inc(consts, 1)
                    linear(0, 0, 0, q_mm)
                    linear(0, 0, 1, k_mm)
                    dve.wait_ge(cleared, 2 + 4 * NQ)
                    v_out(0, 0)

                def body(it, s, first, last):
                    n = it * 2 + s
                    for h in range(HEADS):
                        k = n * HEADS + h
                        if h == 0 and not last:
                            normalise(n + 1)
                        if not (first and h < 1):
                            mask(k - 1, (h - 1) % HEADS)
                        if h % QH == 2 and not (first and h == 2):
                            denominators(n if h > 2 else n - 1, (h // QH - 1) % NQ)
                        if h % QH == 3 and not (first and h == 3):
                            invert(n if h > 3 else n - 1, (h // QH - 1) % NQ)
                        if h in (8, 12):
                            quotient(s, n, h // QH - 2)
                        if h in (0, 4) and not first:
                            quotient(1 - s, n - 1, h // QH + 2)
                        if h == 6 and not first:
                            proj_out(n - 1)
                        if h == 9 and not first:
                            stats.take(dve, n - 1, h_done, n)
                        if not last:
                            if h == 8:
                                low_x(n + 1)
                            if h == 10:
                                linear(1 - s, n + 1, 0, q_mm)
                            if h == 13:
                                linear(1 - s, n + 1, 1, k_mm)
                            if h == 14:
                                v_out(1 - s, n + 1)

                def finish():
                    mask(B * HEADS - 1, HEADS - 1)
                    quotient(1, B - 1, NQ - 2)
                    denominators(B - 1, NQ - 1)
                    invert(B - 1, NQ - 1)
                    quotient(1, B - 1, NQ - 1)
                    proj_out(B - 1)
                    stats.take(dve, B - 1, h_done, B)

                run(dve, start, body, finish)

            @block.scalar
            def _(act):
                def xt_out(m):
                    act.wait_ge(xt_mm, m + 1)
                    since(act, v_mm, m)
                    nc.scalar.activation(xh[:, :, :], F[1][:, 0:DK * S].rearrange("p (k t) -> p k t", k=DK), ACT.Copy).then_inc(xt_evac, 1)

                def squares(s, m, which, mm):
                    act.wait_ge(mm, m + 1)
                    since(act, z_low, (m - 1) * 2 + which + 1)
                    for g in range(G):
                        for half in range(2):
                            src = slice(half * HP, (half + 1) * HP)
                            nc.scalar.activation(z[HP:P, which, 2 * g + half, :], F[which][src, g * S:(g + 1) * S], ACT.Square,
                                                 bias=bias4[src, which, g:g + 1], scale=HD ** -0.5).then_inc(sq_out, 1)

                def high_z(s, m, which):
                    act.wait_ge(lin_out, m * 2 * LIN + (which + 1) * LIN)
                    act.wait_ge(sq_out, m * 2 * LIN + (which + 1) * LIN)
                    since(act, phi_mm, (m - 1) * HEADS)
                    nc.scalar.activation(zh[s][:, which, :, :], z[:, which, :, :], ACT.Copy).then_inc(z_high, 1)

                def start():
                    xt_out(0)
                    act.wait_ge(consts, 1)
                    squares(0, 0, 0, q_mm)
                    squares(0, 0, 1, k_mm)
                    high_z(0, 0, 0)
                    high_z(0, 0, 1)

                def body(it, s, first, last):
                    n = it * 2 + s
                    for h in range(HEADS):
                        k = n * HEADS + h
                        act.wait_ge(phi_mm, k + 1)
                        since(act, att_mm, k - 1)
                        nc.scalar.activation(phi[h % 2][:, :, :], phi_ps[h % 2][:, 0:2 * S].rearrange("p (c t) -> p c t", c=2), ACT.Exp).then_inc(exped, 1)
                        if not last:
                            if h == 7:
                                xt_out(n + 1)
                            if h == 9:
                                squares(1 - s, n + 1, 0, q_mm)
                            if h == 11:
                                high_z(1 - s, n + 1, 0)
                            if h == 12:
                                squares(1 - s, n + 1, 1, k_mm)
                            if h == 14:
                                high_z(1 - s, n + 1, 1)

                run(act, start, body, lambda: None)

            @block.tensor
            def _(pe):
                def xt_in(m):
                    pe.wait_ge(xn_done, m * 2 + 2)
                    since(pe, lin_out, m * 2 * LIN)
                    since(pe, proj_evac, m - 1)
                    for k in range(DK):
                        for t in range(2):
                            last = nc.tensor.transpose(F[1][:, k * S + t * ROWS:k * S + (t + 1) * ROWS], xn[0:ROWS, t, k * P:(k + 1) * P], ident[0:ROWS, 0:ROWS])
                    last.then_inc(xt_mm, 1)

                def qk_in(n, bank, mm, m):
                    pe.wait_ge(x_low, m + 1)
                    if bank == 0:
                        since(pe, v_evac, m * NQ)
                    for g in range(G):
                        terms = [(a, x, k) for k in range(DK) for a, x in three((wh, wl), (xh, xl))]
                        for i, (a, x, k) in enumerate(terms):
                            last = nc.tensor.matmul(F[bank][:, g * S:(g + 1) * S], a[:, k, n, g * P:(g + 1) * P], x[:, k, :], start=(i == 0), stop=(i == len(terms) - 1))
                    last.then_inc(mm, 1)

                def v_in(m):
                    pe.wait_ge(lin_out, m * 2 * LIN + LIN)
                    for t in range(2):
                        terms = [(x, a, k) for k in range(DK) for x, a in three((xh, xl), (wh, wl))]
                        for i, (x, a, k) in enumerate(terms):
                            last = nc.tensor.matmul(F[0][0:ROWS, t * D:(t + 1) * D], x[:, k, t * ROWS:(t + 1) * ROWS], a[:, k, V, :], start=(i == 0), stop=(i == len(terms) - 1))
                    last.then_inc(v_mm, 1)

                def features(s, n, k, h):
                    if h == 0:
                        pe.wait_ge(z_low, (n + 1) * 2)
                    since(pe, exped, k - 1)
                    for i, (w, x) in enumerate(three((omega_h, omega_l), (zh[s], zl[s]))):
                        last = nc.tensor.matmul(phi_ps[h % 2][:, 0:2 * S].rearrange("p (c t) -> p c t", c=2), w[:, h % QH, :], x[:, :, h // QH, :], start=(i == 0), stop=(i == 2))
                    last.then_inc(phi_mm, 1)

                def attend(k, h):
                    pe.wait_ge(exped, k + 1)
                    since(pe, masked, k - 1)
                    q, key = phi[h % 2][:, 0, :], phi[h % 2][:, 1, :]
                    nc.tensor.matmul(att_ps[h % 2][0:ROWS, 0:S], key[:, 0:ROWS], q, start=True, stop=True)
                    nc.tensor.matmul(att_ps[h % 2][0:ROWS, S:S + ROWS], key[:, ROWS:S], q[:, ROWS:S], start=True, stop=True).then_inc(att_mm, 1)

                def values(s, n, k, h):
                    pe.wait_ge(masked, k + 1)
                    qt, hl = h // QH, h % QH
                    if h == 0:
                        pe.wait_ge(v_evac, (n + 1) * NQ)
                    if hl == 0:
                        since(pe, divided, (n * NQ + qt - 1) * 3)
                    head = slice(hl * P, (hl + 1) * P)
                    nc.tensor.matmul(av_ps[qt % 2][:, 0:S], vone[s][0:ROWS, 0, qt, head], att[h % 2][0:ROWS, 0:S], start=(hl == 0), stop=False)
                    nc.tensor.matmul(av_ps[qt % 2][:, ROWS:S], vone[s][0:ROWS, 1, qt, head], att[h % 2][0:ROWS, S:S + ROWS], start=False, stop=(hl == QH - 1)).then_inc(av_mm, 1)

                def proj_in(s, m):
                    pe.wait_ge(y_split, (m + 1) * 4)
                    pe.wait_ge(lin_out, (m + 2) * 2 * LIN if not isinstance(m, int) or m < B - 1 else B * 2 * LIN)
                    for t in range(2):
                        terms = [(y, a, g) for g in range(G) for y, a in three((yh, yl), (wh, wl))]
                        for i, (y, a, g) in enumerate(terms):
                            last = nc.tensor.matmul(F[1][0:ROWS, t * D:(t + 1) * D], y[:, g, t * ROWS:(t + 1) * ROWS], a[:, g, O, :], start=(i == 0), stop=(i == len(terms) - 1))
                    last.then_inc(proj_mm, 1)

                def start():
                    xt_in(0)
                    pe.wait_ge(w_split, 2)
                    qk_in(Q, 0, q_mm, 0)
                    pe.wait_ge(w_split, 4)
                    qk_in(K, 1, k_mm, 0)
                    pe.wait_ge(w_split, 6)
                    v_in(0)
                    pe.wait_ge(consts, 3)
                    pe.wait_ge(wo_split, 2)

                def body(it, s, first, last):
                    n = it * 2 + s
                    for h in range(HEADS):
                        k = n * HEADS + h
                        features(s, n, k, h)
                        if not (first and h < 1):
                            attend(k - 1, (h - 1) % HEADS)
                        if not (first and h < 2):
                            values(s if h >= 2 else 1 - s, n if h >= 2 else n - 1, k - 2, (h - 2) % HEADS)
                        if h == 6 and not first:
                            proj_in(1 - s, n - 1)
                        if not last and h in SIDE:
                            step = SIDE[h]
                            if step == "xt":
                                xt_in(n + 1)
                            if step == "q":
                                qk_in(Q, 0, q_mm, n + 1)
                            if step == "k":
                                qk_in(K, 1, k_mm, n + 1)
                            if step == "v":
                                v_in(n + 1)

                def finish():
                    last = B * HEADS
                    attend(last - 1, HEADS - 1)
                    values(1, B - 1, last - 2, HEADS - 2)
                    values(1, B - 1, last - 1, HEADS - 1)
                    proj_in(1, B - 1)

                run(pe, start, body, finish)


E1, F1 = 8, 1024
FT = F1 // P
THRESH = 1e-9
def stage_gates(nc, io, H, mv, rstd, xh, xl, logit, ident, first_load, first_split):
    with Stage(nc, "ga") as st:
        sb, ps, sem = st.sb, st.ps, st.sem
        wr, br = sb("wr", [P, DK, E1]), sb("br", [P, 1])
        wrh, wrl = sb("wrh", [P, DK, E1], R32), sb("wrl", [P, DK, E1], R32)
        xn = [sb(f"xn{s}", [P, CTILES, D]) for s in range(2)]
        across = sb("across", [P, B * S])
        xt_ps = [ps(f"xt_ps{s}", [P, DK, 512]) for s in range(2)]
        across_ps, logit_ps = [ps(f"across_ps{s}", [P, 512]) for s in range(2)], ps("logit_ps", [P, TILES, E1])
        loaded, wr_split, xn_done, xt_mm, high_out, low_out, across_mm, across_out, logit_mm, logit_out = (
            sem(n) for n in ("loaded", "wr_split", "xn_done", "xt_mm", "high_out", "low_out", "across_mm", "across_out", "logit_mm", "logit_out"))

        def run(eng, body, finish=lambda: None):
            body(0, 0, True)
            body(0, 1, False)
            with eng.Fori(1, NCHUNK // 2) as it:
                body(it, 0, False)
                body(it, 1, False)
            finish()

        with nc.Block() as block:

            @block.sync
            def _(sp):
                sp.dma_start(wr[:, :, :], io["ga_wr"].rearrange("(k p) e -> p k e", p=P)).then_inc(loaded, 16)
                sp.dma_start(br[0:E1, :], io["ga_br"]).then_inc(loaded, 16)
                first_load(sp)

            @block.gpsimd
            def _(pool):
                first_split(pool)

            @block.vector
            def _(dve):
                def low_parts(s, j):
                    dve.wait_ge(high_out, j + 1)
                    tok = ds(j * CHUNK, CHUNK)
                    split_low(nc.vector, xl[:, :, tok], xt_ps[s][:, :, 0:CHUNK], xh[:, :, tok]).then_inc(low_out, 1)

                def normalise(s, j):
                    since(dve, xt_mm, j - 1)
                    for t in range(CTILES):
                        normalise_rows(nc, H, mv, rstd, xn[s][0:ROWS, t, :], j * CTILES + t).then_inc(xn_done, 1)

                def body(it, s, first):
                    j = it * 2 + s
                    normalise(s, j)
                    if first:
                        dve.wait_ge(loaded, 32)
                        split_high(nc.vector, wrh[:, :, :], wr[:, :, :]).then_inc(wr_split, 1)
                        dve.wait_ge(wr_split, 1)
                        split_low(nc.vector, wrl[:, :, :], wr[:, :, :], wrh[:, :, :]).then_inc(wr_split, 1)
                    else:
                        low_parts(1 - s, j - 1)

                run(dve, body, lambda: low_parts(1, NCHUNK - 1))
                dve.wait_ge(logit_mm, 1)
                nc.vector.tensor_copy(logit[0:ROWS, :, :], logit_ps[0:ROWS, :, :]).then_inc(logit_out, 1)

            @block.scalar
            def _(act):
                def biased(s, j):
                    act.wait_ge(across_mm, j + 1)
                    nc.scalar.activation(across[0:E1, ds(j * CHUNK, CHUNK)], across_ps[s][0:E1, 0:CHUNK], ACT.Identity, bias=br[0:E1, 0:1]).then_inc(across_out, 1)

                def body(it, s, first):
                    j = it * 2 + s
                    act.wait_ge(xt_mm, j + 1)
                    nc.scalar.activation(xh[:, :, ds(j * CHUNK, CHUNK)], xt_ps[s][:, :, 0:CHUNK], ACT.Copy).then_inc(high_out, 1)
                    if not first:
                        biased(1 - s, j - 1)

                act.wait_ge(loaded, 32)
                run(act, body, lambda: biased(1, NCHUNK - 1))

            @block.tensor
            def _(pe):
                def logits_in(s, j):
                    pe.wait_ge(low_out, j + 1)
                    since(pe, across_out, j - 1)
                    tok = ds(j * CHUNK, CHUNK)
                    terms = [(w, x, k) for k in range(DK) for w, x in three((wrh, wrl), (xh, xl))]
                    for i, (w, x, k) in enumerate(terms):
                        last = nc.tensor.matmul(across_ps[s][0:E1, 0:CHUNK], w[:, k, :], x[:, k, tok], start=(i == 0), stop=(i == len(terms) - 1))
                    last.then_inc(across_mm, 1)

                def body(it, s, first):
                    j = it * 2 + s
                    pe.wait_ge(xn_done, (j + 1) * CTILES)
                    since(pe, low_out, j - 1)
                    for k in range(DK):
                        for t in range(CTILES):
                            last = nc.tensor.transpose(xt_ps[s][:, k, t * ROWS:(t + 1) * ROWS], xn[s][0:ROWS, t, k * P:(k + 1) * P], ident[0:ROWS, 0:ROWS])
                    last.then_inc(xt_mm, 1)
                    if first:
                        pe.wait_ge(wr_split, 2)
                    else:
                        logits_in(1 - s, j - 1)

                run(pe, body, lambda: logits_in(1, NCHUNK - 1))
                pe.wait_ge(across_out, NCHUNK)
                for tile in range(TILES):
                    last = nc.tensor.transpose(logit_ps[0:ROWS, tile, :], across[0:E1, tile * ROWS:(tile + 1) * ROWS], ident[0:E1, 0:E1])
                last.then_inc(logit_mm, 1)


def entmax(nc, dve, st, chain, root, take_root, logit, gate):
    r, v = slice(0, ROWS), nc.vector
    ranked, cut = st.sb("ranked", [P, TILES, E1]), st.sb("cut", [P, TILES, E1])
    total = st.sb("total", [P, 2, TILES, E1])
    inverse = st.sb("inverse", [P, E1])
    tau, mass, slope = (st.sb(n, [P, TILES]) for n in ("tau", "mass", "slope"))
    wide = lambda t: t[r, :].unsqueeze(2).broadcast_to([ROWS, TILES, E1])
    per_k = inverse[r, :].unsqueeze(1).broadcast_to([ROWS, TILES, E1])
    count = 0

    def step(ins):
        nonlocal count
        count += 1
        ins.then_inc(chain, 1)
        dve.wait_ge(chain, count)

    def over(x):
        step(v.tensor_tensor(cut[r, :, :], x, wide(tau), ALU.subtract))
        step(v.tensor_scalar(cut[r, :, :], cut[r, :, :], 0.0, None, ALU.max))

    for k in range(E1):
        step(v.memset(inverse[:, k:k + 1], 1.0 / (k + 1)))
    for t in range(TILES):
        ins = v.max(ranked[r, t, :], logit[r, t, :])
        count += 1
        ins.then_inc(chain, 1)
    dve.wait_ge(chain, count)
    top = ranked[r, :, 0:1].broadcast_to([ROWS, TILES, E1])
    step(v.tensor_tensor(logit[r, :, :], logit[r, :, :], top, ALU.subtract))
    step(v.tensor_tensor(total[r, 0, :, :], ranked[r, :, :], top, ALU.subtract))
    step(v.tensor_scalar(logit[r, :, :], logit[r, :, :], 0.5, None, ALU.mult))
    step(v.tensor_scalar(ranked[r, :, :], total[r, 0, :, :], 0.5, -1.0, ALU.mult, ALU.max))
    step(v.tensor_copy(total[r, 0, :, :], ranked[r, :, :]))
    step(v.tensor_tensor(total[r, 1, :, :], ranked[r, :, :], ranked[r, :, :], ALU.mult))
    for k in range(1, E1):
        step(v.tensor_tensor(total[r, :, :, k], total[r, :, :, k], total[r, :, :, k - 1], ALU.add))
    step(v.tensor_tensor(total[r, 0, :, :], total[r, 0, :, :], per_k, ALU.mult))
    step(v.tensor_scalar(total[r, 1, :, :], total[r, 1, :, :], -1.0, 1.0, ALU.mult, ALU.add))
    step(v.tensor_tensor(total[r, 1, :, :], total[r, 1, :, :], per_k, ALU.mult))
    step(v.tensor_tensor(root[r, :, :], total[r, 0, :, :], total[r, 0, :, :], ALU.mult))
    step(v.tensor_tensor(root[r, :, :], root[r, :, :], total[r, 1, :, :], ALU.add))
    step(v.tensor_scalar(root[r, :, :], root[r, :, :], 0.0, None, ALU.max))
    take_root()
    step(v.tensor_tensor(total[r, 0, :, :], total[r, 0, :, :], root[r, :, :], ALU.subtract))
    step(v.tensor_tensor(cut[r, :, :], ranked[r, :, :], total[r, 0, :, :], ALU.is_ge))
    step(v.scalar_tensor_tensor(cut[r, :, :], total[r, 0, :, :], 1.0, cut[r, :, :], ALU.add, ALU.mult))
    step(v.tensor_reduce(tau[r, :], cut[r, :, :], AX.X, ALU.max))
    step(v.tensor_scalar(tau[r, :], tau[r, :], -1.0, None, ALU.add))
    over(logit[r, :, :])
    step(v.tensor_tensor(ranked[r, :, :], cut[r, :, :], cut[r, :, :], ALU.mult))
    step(v.tensor_reduce(mass[r, :], ranked[r, :, :], AX.X, ALU.add))
    step(v.tensor_reduce(slope[r, :], cut[r, :, :], AX.X, ALU.add))
    step(v.reciprocal(slope[r, :], slope[r, :]))
    step(v.tensor_scalar(mass[r, :], mass[r, :], -1.0, 0.5, ALU.add, ALU.mult))
    step(v.tensor_tensor(mass[r, :], mass[r, :], slope[r, :], ALU.mult))
    step(v.tensor_tensor(tau[r, :], tau[r, :], mass[r, :], ALU.add))
    over(logit[r, :, :])
    step(v.tensor_tensor(ranked[r, :, :], cut[r, :, :], cut[r, :, :], ALU.mult))
    step(v.tensor_reduce(mass[r, :], ranked[r, :, :], AX.X, ALU.add))
    step(v.reciprocal(mass[r, :], mass[r, :]))
    step(v.tensor_tensor(cut[r, :, :], ranked[r, :, :], wide(mass), ALU.mult))
    step(v.scalar_tensor_tensor(gate[r, :, :], cut[r, :, :], THRESH, cut[r, :, :], ALU.is_gt, ALU.mult))


def stage_gated(nc, io, H, mv, rstd, ident, out):
    with Stage(nc, "gm") as st:
        sb, ps, sem = st.sb, st.ps, st.sem
        xh, xl = sb("xh", [P, DK, B * S], R32), sb("xl", [P, DK, B * S], R32)
        logit, root = sb("logit", [P, TILES, E1]), sb("root", [P, TILES, E1])
        raw1, raw2 = sb("raw1", [P, DK, F1]), sb("raw2", [P, FT, D])
        w1h, w1l = sb("w1h", [P, DK, F1], R32), sb("w1l", [P, DK, F1], R32)
        w2h, w2l = sb("w2h", [P, FT, D], R32), sb("w2l", [P, FT, D], R32)
        b1, b2 = sb("b1", [P, E1, FT]), sb("b2", [P, E1, D])
        gate = sb("gate", [P, TILES, E1])
        b_loaded, raw1_loaded, raw2_loaded = sem("b_loaded"), sem("raw1_loaded"), sem("raw2_loaded")
        w1_split, w2_split, chain, prepared = sem("w1_split"), sem("w2_split"), sem("chain"), sem("prepared")
        root_ready, root_taken = sem("root_ready"), sem("root_taken")
        up_mm, relued, halved, split, down_mm, added, biased, stored, paused = (
            sem(n) for n in ("up_mm", "relued", "halved", "split", "down_mm", "added", "biased", "stored", "paused"))
        BANKS, HIDS, DOWNS = 4, 2, CTILES

        def load(sp, e):
            since(sp, w1_split, e * 2)
            sp.dma_start(raw1[:, :, :], io["gm_w1"][ds(e, 1), :, :].rearrange("o (k p) f -> p (o k) f", p=P)).then_inc(raw1_loaded, 16)
            since(sp, w2_split, e * 2)
            sp.dma_start(raw2[:, :, :], io["gm_w2"][ds(e, 1), :, :].rearrange("o (k p) f -> p (o k) f", p=P)).then_inc(raw2_loaded, 16)

        def first_split(pool):
            for raw, high, low, got, done in ((raw1, w1h, w1l, raw1_loaded, w1_split), (raw2, w2h, w2l, raw2_loaded, w2_split)):
                pool.wait_ge(got, 16)
                split_high(nc.gpsimd, high[:, :, :], raw[:, :, :]).then_inc(done, 1)
                pool.wait_ge(done, 1)
                split_low(nc.gpsimd, low[:, :, :], raw[:, :, :], high[:, :, :]).then_inc(done, 1)

        stage_gates(nc, io, H, mv, rstd, xh, xl, logit, ident, lambda sp: load(sp, 0), first_split)
        hid = [sb(f"hid{i}", [P, CHUNK]) for i in range(2)]
        hh, hl = sb("hh", [P, FT, CHUNK], R32), sb("hl", [P, FT, CHUNK], R32)
        up = [ps(f"up{i}", [P, 512]) for i in range(4)]
        down = [ps(f"down{i}", [P, 512]) for i in range(CTILES)]

        def experts(eng, body, prepare=lambda e: None, between=lambda e: None):
            with eng.Fori(0, E1 - 1) as e:
                prepare(e)
                with eng.Fori(0, NCHUNK) as j:
                    body(e, j, e * NCHUNK + j)
                between(e + 1)
            prepare(E1 - 1)
            with eng.Fori(0, NCHUNK) as j:
                body(E1 - 1, j, (E1 - 1) * NCHUNK + j)

        with nc.Block() as block:

            @block.sync
            def _(sp):
                sp.dma_start(b1[:, :, :], io["gm_b1"].rearrange("p (e f) -> p e f", e=E1)).then_inc(b_loaded, 16)
                sp.dma_start(b2[:, :, :].rearrange("p e d -> p (e d)"), io["gm_b2"].broadcast_to([P, E1 * D])).then_inc(b_loaded, 16)

                with sp.Fori(1, E1) as e:
                    load(sp, e)
                out_v = out.rearrange("b (t p) d -> p (b t) d", p=ROWS)
                for j in range(NCHUNK):
                    sp.wait_ge(added, BANKS + ((E1 - 1) * NCHUNK + j + 1) * CTILES)
                    tiles = slice(j * CTILES, (j + 1) * CTILES)
                    sp.dma_start(out_v[:, tiles, :], H[0:ROWS, tiles, :]).then_inc(stored, 16)
                sp.wait_ge(stored, 16 * NCHUNK)

            @block.gpsimd
            def _(pool):
                with pool.Fori(1, E1) as e:
                    for raw, high, low, done in ((raw1, w1h, w1l, w1_split), (raw2, w2h, w2l, w2_split)):
                        pool.wait_ge(done, e * 2 + 1)
                        split_low(nc.gpsimd, low[:, :, :], raw[:, :, :], high[:, :, :]).then_inc(done, 1)

            @block.vector
            def _(dve):
                dve.sem_inc(split, HIDS)
                dve.sem_inc(added, BANKS)

                def take_root():
                    dve.sem_inc(root_ready, 1)
                    dve.wait_ge(root_taken, 1)

                entmax(nc, dve, st, chain, root, take_root, logit, gate)
                dve.wait_ge(b_loaded, 32)

                def body(e, j, c):
                    for f in range(FT):
                        k = c * FT + f
                        dve.wait_ge(relued, k + 1 + BANKS)
                        if f == 0:
                            dve.wait_ge(down_mm, c * CTILES + DOWNS)
                        split_high(nc.vector, hh[:, f, :], hid[f % 2][:, :]).then_inc(halved, 1)
                        dve.wait_ge(halved, k + 1)
                        split_low(nc.vector, hl[:, f, :], hid[f % 2][:, :], hh[:, f, :]).then_inc(split, 1)
                    for t in range(CTILES):
                        tile = j * CTILES + t
                        row = H[0:ROWS, ds(tile, 1), :].rearrange("p a d -> p (a d)")
                        g = gate[0:ROWS, ds(tile, 1), ds(e, 1)].rearrange("p a e -> p (a e)")
                        nc.vector.scalar_tensor_tensor(row, b2[0:ROWS, ds(e, 1), :].rearrange("p a d -> p (a d)"), g, row, ALU.mult, ALU.add).then_inc(biased, 1)
                    for t in range(CTILES):
                        tile = j * CTILES + t
                        row = H[0:ROWS, ds(tile, 1), :].rearrange("p a d -> p (a d)")
                        g = gate[0:ROWS, ds(tile, 1), ds(e, 1)].rearrange("p a e -> p (a e)")
                        dve.wait_ge(biased, c * CTILES + t + 1)
                        dve.wait_ge(down_mm, c * CTILES + t + 1 + DOWNS)
                        nc.vector.scalar_tensor_tensor(row, down[t][0:ROWS, 0:D], g, row, ALU.mult, ALU.add).then_inc(added, 1)

                experts(dve, body)

            @block.scalar
            def _(act):
                act.sem_inc(relued, BANKS)
                act.wait_ge(root_ready, 1)
                nc.scalar.activation(root[0:ROWS, :, :], root[0:ROWS, :, :], ACT.Sqrt).then_inc(root_taken, 1)
                act.wait_ge(b_loaded, 32)

                def body(e, j, c):
                    for f in range(FT):
                        k = c * FT + f
                        act.wait_ge(up_mm, k + 1)
                        act.wait_ge(split, k + 1)
                        nc.scalar.activation(hid[f % 2][:, :], up[f % 4][:, 0:CHUNK], ACT.Relu,
                                             bias=b1[:, ds(e, 1), f:f + 1].rearrange("p a f -> p (a f)")).then_inc(relued, 1)

                def between(e):
                    act.wait_ge(raw1_loaded, e * 16 + 16)
                    act.wait_ge(up_mm, e * NCHUNK * FT)
                    nc.scalar.activation(w1h[:, :, :], raw1[:, :, :], ACT.Copy).then_inc(w1_split, 1)
                    act.wait_ge(raw2_loaded, e * 16 + 16)
                    act.wait_ge(down_mm, DOWNS + e * NCHUNK * CTILES)
                    nc.scalar.activation(w2h[:, :, :], raw2[:, :, :], ACT.Copy).then_inc(w2_split, 1)

                experts(act, body, between=between)

            @block.tensor
            def _(pe):
                pe.sem_inc(down_mm, DOWNS)

                def prepare(e):
                    pause(pe, w1_split, e * 2 + 2, prepared)

                def body(e, j, c):
                    tok = ds(j * CHUNK, CHUNK)
                    for f in range(FT):
                        k = c * FT + f
                        pe.wait_ge(relued, k + 1)
                        cols = slice(f * P, (f + 1) * P)
                        terms = [(w, x, kk) for kk in range(DK) for w, x in three((w1h, w1l), (xh, xl))]
                        for i, (w, x, kk) in enumerate(terms):
                            last = nc.tensor.matmul(up[f % 4][:, 0:CHUNK], w[:, kk, cols], x[:, kk, tok], start=(i == 0), stop=(i == len(terms) - 1))
                        last.then_inc(up_mm, 1)
                    pe.wait_ge(w2_split, e * 2 + 2)
                    for t in range(CTILES):
                        rows = slice(t * ROWS, (t + 1) * ROWS)
                        pe.wait_ge(added, c * CTILES + t + 1)
                        for f in range(FT):
                            if t == 0:
                                pe.wait_ge(split, c * FT + f + 1 + HIDS)
                            for i, (h, w) in enumerate(three((hh, hl), (w2h, w2l))):
                                last = nc.tensor.matmul(down[t][0:ROWS, 0:D], h[:, f, rows], w[:, f, :], start=(f == 0 and i == 0), stop=(f == FT - 1 and i == 2))
                        last.then_inc(down_mm, 1)

                experts(pe, body, prepare)


def build(nc, io, out):
    with ExitStack() as ctx:
        H = ctx.enter_context(nc.sbuf_tensor("H", [P, TILES, D], F32))
        mv = ctx.enter_context(nc.sbuf_tensor("mv", [P, TILES, 2], F32))
        rstd = ctx.enter_context(nc.sbuf_tensor("rstd", [P, TILES], F32))
        ident = ctx.enter_context(nc.sbuf_tensor("ident", [P, P], F32))
        stage_attention(nc, io, H, mv, rstd, ident)
        stage_rstd(nc, "r1", mv, rstd)
        stage_routed(nc, io, H, mv, rstd, ident)
        stage_rstd(nc, "r2", mv, rstd)
        stage_features(nc, io, H, mv, rstd, ident)
        stage_rstd(nc, "r3", mv, rstd)
        stage_gated(nc, io, H, mv, rstd, ident, out)


def layout(i):
    a = {k: np.asarray(v) for k, v in i.items()}
    zeros = lambda *s: np.zeros(s, np.float32)
    io = {}
    io["xt"] = a["x"].reshape(B * S, PATCH).T
    io["tok_in"] = np.concatenate([
        np.concatenate([a["L0_tok_W_h"].T, a["L0_tok_b_h"][None], zeros(1, HID)], 0),
        np.concatenate([a["L0_tok_W_r"].T, a["L0_tok_b_r"][None], a["L0_tok_b_o"][None]], 0)], 1)
    io["tok_out"] = a["L0_tok_W_o"].T
    io["ident"] = np.eye(P, dtype=np.float32)
    for k in "qkvo":
        io[f"at_w{k}"] = a[f"L0_attn_W{k}"]
    for k in "qk":
        io[f"at_b{k}"] = a[f"L0_attn_b{k}"].reshape(G, P).T
    for k in "vo":
        io[f"at_b{k}"] = a[f"L0_attn_b{k}"][None]
    rel = np.concatenate([a["L0_attn_rel_key"], zeros(P, HD)], 0)
    first = RANGE - 1 - (S - 2)
    io["at_relx"] = np.concatenate([rel[first - r:first - r + RELN].T for r in range(XR)], 0)
    p = np.arange(P)
    r, j = np.arange(BLK)[:, None], np.arange(MINW)[None]
    tri = np.concatenate([np.where(j > r + late, MASKED, 0.0) for late in (0, BLK)], 1)
    io["at_cst"] = np.concatenate([
        p[:, None] // HD == np.arange(GH), p[:, None] // HD == np.arange(BLK) % XR,
        np.pad(r == p % BLK, ((0, P - BLK), (0, 0))), np.pad(tri, ((0, P - BLK), (0, 0)))], 1).astype(np.float32)
    io["rt_wr"], io["rt_br"] = a["L0_ffn_router_w"].T, a["L0_ffn_router_b"][None]
    io["rt_ids"] = np.arange(E0, dtype=np.float32)[None]
    io["rt_own"] = np.repeat(np.eye(E0, dtype=np.float32), H0, 1)
    io["rt_w1"] = a["L0_ffn_weights1"].transpose(1, 0, 2).reshape(D, E0 * H0)
    io["rt_w2"] = a["L0_ffn_weights2"].reshape(E0 * H0, D)
    io["rt_b1"] = a["L0_ffn_bias1"].reshape(PR, P).T
    io["rt_b2"] = np.concatenate([a["L0_ffn_bias2"], zeros(P - E0, D)], 0)
    w, bias = a["L1_attn_W_attn"], a["L1_attn_b_attn"]
    io["fe_w"], io["fe_wo"] = w, a["L1_attn_W_proj"]
    io["fe_bias"] = bias[:2 * D].reshape(2 * G, P).T
    io["fe_bv"], io["fe_bo"] = bias[None, 2 * D:], a["L1_attn_b_proj"][None]
    om = zeros(2, QH, HD, QH, M)
    for h in range(QH):
        om[0, h, :, h, :] = a["L1_attn_omega"]
        om[1, h, :, h, :] = -0.5
    io["fe_omega"] = om.reshape(P, QH * M)
    s_, t_ = np.arange(ROWS)[:, None], np.arange(S)[None]
    io["fe_causal"] = np.concatenate([s_ <= t_, s_ <= t_[:, :ROWS]], 1).astype(np.float32)
    io["ga_wr"], io["ga_br"] = a["L1_ffn_Wr"], a["L1_ffn_br"][:, None]
    io["gm_w1"], io["gm_w2"] = a["L1_ffn_W1"], a["L1_ffn_W2"]
    io["gm_b1"] = a["L1_ffn_b1"].reshape(E1 * FT, P).T
    io["gm_b2"] = a["L1_ffn_b2"].reshape(1, E1 * D)
    return {k: np.ascontiguousarray(v) for k, v in io.items()}


def kernel(**inputs):
    import concourse.bacc as bacc
    from concourse.bass_utils import run_bass_kernel_spmd

    nc = bacc.Bacc("TRN2", target_bir_lowering=False, num_devices=1)
    arrays = layout(inputs)
    io = {k: nc.dram_tensor(f"in_{k}", v.shape, mybir.dt.from_np(v.dtype), kind="ExternalInput").ap() for k, v in arrays.items()}
    out = nc.dram_tensor("out", (B, S, D), F32, kind="ExternalOutput").ap()
    build(nc, io, out)
    r = run_bass_kernel_spmd(nc, [{f"in_{k}": v for k, v in arrays.items()}], core_ids=[0])
    return r.results[0]["out"]
```
